# Optimizing a Trainium2 kernel written in Bass

```python
import numpy as np
import jax
import jax.numpy as jnp

def _softmax(x, axis=-1):
    return jax.nn.softmax(x, axis=axis)

def _gelu(x):
    return jax.nn.gelu(x, approximate=True)

def _silu(x):
    return jax.nn.silu(x)

def _sigmoid(x):
    return jax.nn.sigmoid(x)

def _layernorm(x, axis=-1, eps=1e-05):
    m = jnp.mean(x, axis=axis, keepdims=True)
    v = jnp.var(x, axis=axis, keepdims=True)
    return (x - m) / jnp.sqrt(v + eps)

def _scatter_add(tgt, idx, src, axis=0):
    return tgt.at[idx].add(src)

def _segment_sum(src, seg, n):
    return jax.ops.segment_sum(src, seg, n)
kernel_name = 'mk_xattn_ffn_d1_seqx_r4_f18d63'

def setup_inputs(seed: int=0):
    np.random.seed(seed)
    _w = jnp.asarray

    def _rec_inputs():
        import jax
        import jax.numpy as jnp
        _rk = jax.random.key(seed)
        x = -0.000929 + 1 * jax.random.normal(jax.random.fold_in(_rk, 1), (32, 112, 256), jnp.float32)
        _lenS = 112 - jax.random.randint(jax.random.fold_in(_rk, 7), (32,), 0, max(1, 112 // 4) + 1, jnp.int32)
        _lenS2 = 375 - jax.random.randint(jax.random.fold_in(_rk, 8), (32,), 0, max(1, 375 // 4) + 1, jnp.int32)
        _ctx_1024P = jax.random.normal(jax.random.fold_in(_rk, 11), (32, 16, 256), jnp.float32)
        _ctx_1024c = jax.random.dirichlet(jax.random.fold_in(_rk, 511), 0.3 * jnp.ones((16,), jnp.float32), (32, 375))
        _ctx_1024t = jnp.einsum('bsk,bkd->bsd', _ctx_1024c, _ctx_1024P)
        _ctx_1024t = _ctx_1024t * jax.lax.rsqrt(jnp.mean(jnp.square(_ctx_1024t)) + 1e-12) * 0.953939
        ctx_1024 = -1.52775e-05 + 0.999936 * (_ctx_1024t + 0.3 * jax.random.normal(jax.random.fold_in(_rk, 611), (32, 375, 256), jnp.float32))
        return (x, ctx_1024)
    x, ctx_1024 = _rec_inputs()

    def _L0_xattn_setup():
        import jax, jax.numpy as jnp
        import numpy as np
        DIM = 256
        H = 16
        D = 64
        INNER = H * D
        EPS = 1e-05

        def layernorm(x, w, b):
            mu = jnp.mean(x, axis=-1, keepdims=True)
            var = jnp.var(x, axis=-1, keepdims=True)
            return (x - mu) * jax.lax.rsqrt(var + EPS) * w + b
        key = jax.random.key(seed)
        ks = jax.random.split(key, 8)
        B, N, S = (4, 64, 2048)
        s = 1.0 / np.sqrt(DIM)
        return {'latents': jax.random.normal(ks[0], (B, N, DIM), jnp.float32), 'context': jax.random.normal(ks[1], (B, S, DIM), jnp.float32), 'ln_l_w': jnp.ones((DIM,), jnp.float32), 'ln_l_b': jnp.zeros((DIM,), jnp.float32), 'ln_c_w': jnp.ones((DIM,), jnp.float32), 'ln_c_b': jnp.zeros((DIM,), jnp.float32), 'Wq': jax.random.normal(ks[2], (DIM, INNER), jnp.float32) * s, 'Wkv': jax.random.normal(ks[3], (DIM, 2 * INNER), jnp.float32) * s, 'Wo': jax.random.normal(ks[4], (INNER, DIM), jnp.float32) * (1.0 / np.sqrt(INNER)), 'bo': jnp.zeros((DIM,), jnp.float32)}
    _L0_xattn_all = _L0_xattn_setup()
    _L0_xattn_in = {k: v for k, v in _L0_xattn_all.items() if k in ('ln_l_w', 'ln_l_b', 'ln_c_w', 'ln_c_b', 'Wq', 'Wkv', 'Wo', 'bo')}
    del _L0_xattn_all

    def _L0_ffn_setup():
        import jax, jax.numpy as jnp
        import numpy as np
        D_IN, D_HID = (256, 1024)

        def _ternary(key, shape):
            return jax.random.randint(key, shape, -1, 2).astype(jnp.float32)

        def _tlin(x, w, s):
            return jnp.einsum('bsi,oi->bso', x, w) * s
        key = jax.random.key(seed)
        ks = jax.random.split(key, 12)
        inv = lambda fan: 1.0 / np.sqrt(fan).astype(np.float32)
        return {'x': jax.random.normal(ks[0], (4, 512, D_IN), dtype=jnp.float32), 'w1_w': _ternary(ks[1], (D_HID, D_IN)), 'w1_s': jax.random.uniform(ks[2], (D_HID,), dtype=jnp.float32) * inv(D_IN), 'w2_w': _ternary(ks[3], (D_HID, D_IN)), 'w2_s': jax.random.uniform(ks[4], (D_HID,), dtype=jnp.float32) * inv(D_IN), 'h1_w': _ternary(ks[5], (D_HID, D_HID)), 'h1_s': jax.random.uniform(ks[6], (D_HID,), dtype=jnp.float32) * inv(D_HID), 'h2_w': _ternary(ks[7], (D_HID, D_HID)), 'h2_s': jax.random.uniform(ks[8], (D_HID,), dtype=jnp.float32) * inv(D_HID), 'w3_w': _ternary(ks[9], (D_IN, D_HID)), 'w3_s': jax.random.uniform(ks[10], (D_IN,), dtype=jnp.float32) * inv(D_HID)}
    _L0_ffn_all = _L0_ffn_setup()
    _L0_ffn_in = {k: v for k, v in _L0_ffn_all.items() if k in ('w1_w', 'w1_s', 'w2_w', 'w2_s', 'h1_w', 'h1_s', 'h2_w', 'h2_s', 'w3_w', 'w3_s')}
    del _L0_ffn_all
    return {'x': x, 'ctx_1024': ctx_1024, 'L0_xattn_ln_l_w': _L0_xattn_in['ln_l_w'], 'L0_xattn_ln_l_b': _L0_xattn_in['ln_l_b'], 'L0_xattn_ln_c_w': _L0_xattn_in['ln_c_w'], 'L0_xattn_ln_c_b': _L0_xattn_in['ln_c_b'], 'L0_xattn_Wq': _L0_xattn_in['Wq'], 'L0_xattn_Wkv': _L0_xattn_in['Wkv'], 'L0_xattn_Wo': _L0_xattn_in['Wo'], 'L0_xattn_bo': _L0_xattn_in['bo'], 'L0_ffn_w1_w': _L0_ffn_in['w1_w'], 'L0_ffn_w1_s': _L0_ffn_in['w1_s'], 'L0_ffn_w2_w': _L0_ffn_in['w2_w'], 'L0_ffn_w2_s': _L0_ffn_in['w2_s'], 'L0_ffn_h1_w': _L0_ffn_in['h1_w'], 'L0_ffn_h1_s': _L0_ffn_in['h1_s'], 'L0_ffn_h2_w': _L0_ffn_in['h2_w'], 'L0_ffn_h2_s': _L0_ffn_in['h2_s'], 'L0_ffn_w3_w': _L0_ffn_in['w3_w'], 'L0_ffn_w3_s': _L0_ffn_in['w3_s']}

def reference(x, ctx_1024, L0_xattn_ln_l_w, L0_xattn_ln_l_b, L0_xattn_ln_c_w, L0_xattn_ln_c_b, L0_xattn_Wq, L0_xattn_Wkv, L0_xattn_Wo, L0_xattn_bo, L0_ffn_w1_w, L0_ffn_w1_s, L0_ffn_w2_w, L0_ffn_w2_s, L0_ffn_h1_w, L0_ffn_h1_s, L0_ffn_h2_w, L0_ffn_h2_s, L0_ffn_w3_w, L0_ffn_w3_s):
    import jax
    import jax.numpy as jnp

    def _L0_xattn_ref(latents, context, ln_l_w, ln_l_b, ln_c_w, ln_c_b, Wq, Wkv, Wo, bo):
        import jax, jax.numpy as jnp
        import numpy as np
        DIM = 256
        H = 16
        D = 64
        INNER = H * D
        EPS = 1e-05

        def layernorm(x, w, b):
            mu = jnp.mean(x, axis=-1, keepdims=True)
            var = jnp.var(x, axis=-1, keepdims=True)
            return (x - mu) * jax.lax.rsqrt(var + EPS) * w + b
        b, n, _ = latents.shape
        s = context.shape[1]
        lat = layernorm(latents, ln_l_w, ln_l_b)
        ctx = layernorm(context, ln_c_w, ln_c_b)
        q = (lat @ Wq).reshape(b, n, H, D).transpose(0, 2, 1, 3)
        kv = ctx @ Wkv
        k, v = jnp.split(kv, 2, axis=-1)
        k = k.reshape(b, s, H, D).transpose(0, 2, 1, 3)
        v = v.reshape(b, s, H, D).transpose(0, 2, 1, 3)
        scale = D ** (-0.5)
        attn = jnp.einsum('bhnd,bhsd->bhns', q, k) * scale
        attn = jnp.clip(attn, -11.0, 11.0)
        attn = jax.nn.softmax(attn, axis=-1)
        out = jnp.einsum('bhns,bhsd->bhnd', attn, v)
        out = out.transpose(0, 2, 1, 3).reshape(b, n, INNER)
        return out @ Wo + bo

    def _L0_ffn_ref(x, w1_w, w1_s, w2_w, w2_s, h1_w, h1_s, h2_w, h2_s, w3_w, w3_s):
        import jax, jax.numpy as jnp
        import numpy as np
        D_IN, D_HID = (256, 1024)

        def _ternary(key, shape):
            return jax.random.randint(key, shape, -1, 2).astype(jnp.float32)

        def _tlin(x, w, s):
            return jnp.einsum('bsi,oi->bso', x, w) * s
        h = jax.nn.silu(_tlin(x, w1_w, w1_s)) * _tlin(x, w2_w, w2_s)
        h = jax.nn.gelu(_tlin(h, h1_w, h1_s), approximate=False)
        h = jax.nn.gelu(_tlin(h, h2_w, h2_s), approximate=False)
        return _tlin(h, w3_w, w3_s)
    x = x + _L0_xattn_ref(_layernorm(x, axis=-1), ctx_1024, L0_xattn_ln_l_w, L0_xattn_ln_l_b, L0_xattn_ln_c_w, L0_xattn_ln_c_b, L0_xattn_Wq, L0_xattn_Wkv, L0_xattn_Wo, L0_xattn_bo)
    x = x + _L0_ffn_ref(_layernorm(x, axis=-1), L0_ffn_w1_w, L0_ffn_w1_s, L0_ffn_w2_w, L0_ffn_w2_s, L0_ffn_h1_w, L0_ffn_h1_s, L0_ffn_h2_w, L0_ffn_h2_s, L0_ffn_w3_w, L0_ffn_w3_s)
    return x

_drawn_inputs = setup_inputs


def setup_inputs(seed=0):
    import zlib

    import numpy as np

    out = dict(_drawn_inputs(seed))
    spreads = {'L0_xattn_ln_l_w': (1.0, 0.2),
     'L0_xattn_ln_l_b': (0.0, 0.1),
     'L0_xattn_ln_c_w': (1.0, 0.2),
     'L0_xattn_ln_c_b': (0.0, 0.1),
     'L0_xattn_bo': (0.0, 0.1)}
    factors = {}
    for name, (base, spread) in spreads.items():
        noise = np.random.default_rng([zlib.crc32(name.encode()), seed]).standard_normal(out[name].shape)
        drawn = base * np.exp(spread * noise) if base else spread * noise
        out[name] = jnp.asarray(drawn.astype(out[name].dtype))
    for name, factor in factors.items():
        out[name] = (out[name] * factor).astype(out[name].dtype)
    return out
```

```python
from contextlib import ExitStack

import numpy as np

import concourse.bass as bass
from concourse import mybir

ALU = mybir.AluOpType
ACT = mybir.ActivationFunctionType
F32 = mybir.dt.float32
F32R = mybir.dt.float32r
I32 = mybir.dt.int32

B, NQ, DIM = 32, 112, 256
SK, H, D = 375, 16, 64
INNER = H * D
HID = 1024
P = 128
KC = DIM // P
SC, SP_ = 3, SK // 3
SKE = SK + 1
PAIRS = H // 2
QUADS = H // 4
D1 = D + 1
EPS = 1e-5
CLIP = 11.0
LOOPED = B - 2
MAGIC = 1597463007.0
NEWTON = 3

ROWS = B * NQ
TR = 512
TILES = ROWS // TR
RS = TR // P
HC = HID // P

X_UNITS = ["Xx", "X0", "X1"]
V_LOW = ["V00", "V01", "V02"]
V_HIGH = ["V10", "V11", "V12"]
ATTEND = ["O0", "O1", "O2", "O3", "W"]
PRO = X_UNITS + ["K%d" % m for m in range(PAIRS)] + ["Q0", "Q1"] + V_LOW + V_HIGH + X_UNITS
STEADY = (["K0", "K1", "K2", "K3", "O0"] + V_LOW + ["K4", "K5", "O1", "K6", "K7", "O2", "Q0", "Q1"]
          + V_HIGH + X_UNITS + ["O3", "W"])
LATE = [u for u in STEADY if u not in X_UNITS]
ORDER = PRO + STEADY * LOOPED + LATE + ATTEND
READERS = {"K": "AD", "Q": "AD", "O": "AD", "W": "Y", "X": "AD"}


def readers(unit):
    if unit[0] == "V":
        return "AD"[(int(unit[1]) + int(unit[2])) % 2]
    return "A" if unit == "Xx" else READERS[unit[0]]


def prefix(order, engine, which):
    out = [0]
    for u in order:
        out.append(out[-1] + (engine in which(u)))
    return out


BEFORE = {e: prefix(ORDER, e, readers) for e in "ADY"}


def place(it, unit):
    if it == -2:
        return PRO.index(unit)
    if it == -1:
        return len(PRO) - 1 - PRO[::-1].index(unit)
    base = len(PRO) + len(STEADY) * min(it, LOOPED) + (len(LATE) if it > LOOPED else 0)
    names = STEADY if it < LOOPED else LATE if it == LOOPED else ATTEND
    return base + names.index(unit)


def along(it, f, last=LOOPED - 1):
    if isinstance(it, int):
        return f(it)
    step = f(2) - f(1)
    assert all(f(i) == f(1) + step * (i - 1) for i in range(1, last + 1))
    return it * step + (f(1) - step)


def inverse_root(nc, pool, out, var, const, work, newton, first, done):
    v, h, t = work[0], work[1], work[2]
    eps, minus_half, one_half_more = const[0], const[1], const[2]
    pool_ops = nc.gpsimd

    pool_ops.tensor_tensor(v, var, eps, ALU.add).then_inc(newton, 1)
    pool.wait_ge(newton, first + 1)
    pool_ops.tensor_tensor(h, v, minus_half, ALU.mult).then_inc(newton, 1)
    pool_ops.tensor_scalar(out.bitcast(I32), v.bitcast(I32), -0.5, MAGIC, ALU.mult, ALU.add).then_inc(newton, 1)
    for k in range(NEWTON):
        n = first + 3 + 4 * k
        pool.wait_ge(newton, n)
        pool_ops.tensor_tensor(t, out, out, ALU.mult).then_inc(newton, 1)
        pool.wait_ge(newton, n + 1)
        pool_ops.tensor_tensor(t, t, h, ALU.mult).then_inc(newton, 1)
        pool.wait_ge(newton, n + 2)
        pool_ops.tensor_tensor(t, t, one_half_more, ALU.add).then_inc(newton, 1)
        pool.wait_ge(newton, n + 3)
        last = k == NEWTON - 1
        pool_ops.tensor_tensor(out, out, t, ALU.mult).then_inc(done if last else newton, 1)


NEWTON_OPS = 3 + 4 * NEWTON - 1


def later(it):
    return not isinstance(it, int) or it > 0


def attention(nc, io, x1):
    with ExitStack() as ctx:
        def sb(name, shape, dt=F32):
            return ctx.enter_context(nc.sbuf_tensor(name, shape, dt))

        def sem(name):
            return ctx.enter_context(nc.semaphore(name))

        wkv_hi = sb("wkv_hi", [P, KC, 2 * INNER], F32R)
        wkv_lo = sb("wkv_lo", [P, KC, 2 * INNER], F32R)
        wq = sb("wq", [P, KC, INNER])
        wo_hi = sb("wo_hi", [P, PAIRS, DIM], F32R)
        wo_lo = sb("wo_lo", [P, PAIRS, DIM], F32R)
        lnl_w = sb("lnl_w", [P, KC])
        lnl_b = sb("lnl_b", [P, KC])
        lnc_w = sb("lnc_w", [P, KC])
        lnc_b = sb("lnc_b", [P, KC])
        bo_rows = sb("bo_rows", [P, DIM])
        ident = sb("ident", [P, P])
        ctx_in = sb("ctx_in", [SP_, SC, DIM])
        x_in = sb("x_in", [NQ, DIM])
        stats = sb("stats", [P, SC + 1, 6])
        mv = sb("mv", [P, SC + 1, 2])
        x_stats = sb("x_stats", [P, 6])
        x_mv = sb("x_mv", [P, 1, 2])
        rstd = sb("rstd", [P, SC + 1, 1])
        x_rstd = sb("x_rstd", [P, 1, 1])
        const = sb("newton_const", [P, SC + 1, 3])
        work = sb("newton_work", [P, SC + 1, 3])
        x_work = sb("newton_x_work", [P, 1, 3])
        idle = sb("idle", [P, 1])
        ctx_n = sb("ctx_n", [SP_, SC, DIM])
        x_n1 = sb("x_n1", [NQ, DIM])
        x_n2 = sb("x_n2", [NQ, DIM])
        ctx_f = sb("ctx_f", [P, KC, SK])
        ctxT_hi = sb("ctxT_hi", [P, KC, SKE], F32R)
        ctxT_lo = sb("ctxT_lo", [P, KC, SKE], F32R)
        xT = sb("xT", [P, KC, NQ])
        k_hi = sb("k_hi", [P, PAIRS, SK], F32R)
        k_lo = sb("k_lo", [P, PAIRS, SK], F32R)
        q_hi = sb("q_hi", [P, PAIRS, 2 * NQ], F32R)
        q_lo = sb("q_lo", [P, PAIRS, 2 * NQ], F32R)
        v = sb("v", [SP_, SC, H, D1])
        probs = sb("probs", [SP_, 2, SC, 4 * NQ])
        rden = sb("rden", [NQ, 4, 1])
        o = sb("o", [NQ, INNER])
        oT_hi = sb("oT_hi", [P, PAIRS, NQ], F32R)
        oT_lo = sb("oT_lo", [P, PAIRS, NQ], F32R)
        x_res = sb("x_res", [NQ, DIM])
        x_bo = sb("x_bo", [NQ, DIM])
        y = sb("y", [NQ, DIM])

        with ExitStack() as stage:
            raw_kv = stage.enter_context(nc.sbuf_tensor("raw_kv", [P, KC, 2 * INNER], F32))
            raw_o = stage.enter_context(nc.sbuf_tensor("raw_o", [P, PAIRS, DIM], F32))
            kv_in = [sem("kv_in%d" % k) for k in range(KC)]
            wo_in, small_in, direct_in = sem("wo_in"), sem("small_in"), sem("direct_in")
            heads, tails, ones_set, ident_set = sem("heads"), sem("tails"), sem("ones_set"), sem("ident_set")
            scaled = sem("scaled")
            with nc.Block() as block:
                @block.sync
                def _(sp):
                    for k in range(KC):
                        sp.dma_start(raw_kv[:, k, :], io["wkv"][k]).then_inc(kv_in[k], 16)
                    sp.dma_start(raw_o[:], io["wo"]).then_inc(wo_in, 16)
                    sp.dma_start(wq[:], io["wq"]).then_inc(direct_in, 16)
                    sp.dma_start(bo_rows[:], io["bo"].partition_broadcast(P)).then_inc(direct_in, 16)
                    sp.wait_ge(direct_in, 32)

                @block.scalar
                def _(act):
                    for t, name in ((lnl_w, "lnl_w"), (lnl_b, "lnl_b"), (lnc_w, "lnc_w"), (lnc_b, "lnc_b")):
                        act.dma_start(t[:], io[name]).then_inc(small_in, 16)
                    act.wait_ge(small_in, 64)
                    nc.scalar.mul(lnl_w[:], lnl_w[:], float(D) ** -0.5).then_inc(scaled, 1)
                    nc.scalar.mul(lnl_b[:], lnl_b[:], float(D) ** -0.5).then_inc(scaled, 1)
                    for k in range(KC):
                        act.wait_ge(kv_in[k], 16)
                        nc.scalar.copy(wkv_hi[:, k, :], raw_kv[:, k, :]).then_inc(heads, 1)
                    act.wait_ge(wo_in, 16)
                    nc.scalar.copy(wo_hi[:], raw_o[:]).then_inc(heads, 1)

                @block.vector
                def _(dve):
                    nc.vector.memset(mv[:], 1.0).then_inc(ones_set, 1)
                    nc.vector.memset(x_mv[:], 1.0).then_inc(ones_set, 1)
                    for k, c in enumerate((EPS, -0.5, 1.5)):
                        nc.vector.memset(const[:, :, k:k + 1], c).then_inc(ones_set, 1)
                    nc.vector.memset(v[:], 1.0).then_inc(ones_set, 1)
                    for k in range(KC):
                        dve.wait_ge(heads, k + 1)
                        nc.vector.tensor_tensor(wkv_lo[:, k, :], raw_kv[:, k, :], wkv_hi[:, k, :],
                                                ALU.subtract).then_inc(tails, 1)
                    dve.wait_ge(heads, KC + 1)
                    nc.vector.tensor_tensor(wo_lo[:], raw_o[:], wo_hi[:], ALU.subtract).then_inc(tails, 1)

                @block.gpsimd
                def _(pool):
                    nc.gpsimd.memset(ident[:], 0.0).then_inc(ident_set, 1)
                    pool.wait_ge(ident_set, 1)
                    nc.gpsimd.affine_select(out=ident[:], in_=ident[:], compare_op=ALU.not_equal, fill=1.0,
                                            base=0, pattern=[[-1, P]], channel_multiplier=1).then_inc(ident_set, 1)
                    nc.gpsimd.memset(q_hi[:].bitcast(F32), 0.0).then_inc(ident_set, 1)
                    nc.gpsimd.memset(q_lo[:].bitcast(F32), 0.0).then_inc(ident_set, 1)
                    nc.gpsimd.memset(ctxT_hi[:].bitcast(F32), 0.0).then_inc(ident_set, 1)
                    nc.gpsimd.memset(ctxT_lo[:].bitcast(F32), 0.0).then_inc(ident_set, 1)

        shared = ctx.enter_context(nc.psum_tensor("shared", [P, 3, 512], F32))
        scores = ctx.enter_context(nc.psum_tensor("scores", [P, 3, 512], F32))
        mixed = ctx.enter_context(nc.psum_tensor("mixed", [P, 2, 512], F32))

        ctx_loaded, x_loaded = sem("ctx_loaded"), sem("x_loaded")
        stats_done, mv_ready, rstd_ready = sem("stats_done"), sem("mv_ready"), sem("rstd_ready")
        x_normed1, x_stats_done, x_mv_ready = sem("x_normed1"), sem("x_stats_done"), sem("x_mv_ready")
        x_rstd_ready, x_normed2, ctx_normed = sem("x_rstd_ready"), sem("x_normed2"), sem("ctx_normed")
        newton = sem("newton")
        unit_ready = sem("unit_ready")
        act_emptied = sem("act_emptied")
        dve_emptied = sem("dve_emptied")
        affine_done, head_done = sem("affine_done"), sem("head_done")
        scores_ready, exp_done, clipped = sem("scores_ready"), sem("exp_done"), sem("clipped")
        mixed_ready, rden_ready, o_normed = sem("mixed_ready"), sem("rden_ready"), sem("o_normed")
        res_loaded, x_bo_ready, y_ready, stored = sem("res_loaded"), sem("x_bo_ready"), sem("y_ready"), sem("stored")
        emptied = {"A": act_emptied, "D": dve_emptied, "Y": y_ready}

        def wait_emptied(eng, it, unit, engine, back=0):
            eng.wait_ge(emptied[engine], along(it, lambda i: BEFORE[engine][place(i - back, unit) + 1]))

        def bank(it, unit):
            return shared[:, place(it if isinstance(it, int) else 1, unit) % 3, :]

        def wait_unit(eng, it, unit, back=0):
            eng.wait_ge(unit_ready, along(it, lambda i: place(i - back, unit) + 1))

        with nc.Block() as block:
            @block.sync
            def _(sp):
                sp.dma_start(ctx_in[:], io["ctx"][0]).then_inc(ctx_loaded, 16)
                sp.dma_start(x_in[:], io["x"][0]).then_inc(x_loaded, 16)
                with sp.Fori(1, B) as b:
                    sp.wait_ge(ctx_normed, b * SC)
                    sp.dma_start(ctx_in[:], io["ctx"][b]).then_inc(ctx_loaded, 16)
                    sp.wait_ge(x_normed1, b)
                    sp.dma_start(x_in[:], io["x"][b]).then_inc(x_loaded, 16)

            @block.gpsimd
            def _(pool):
                def roots(b):
                    pool.wait_ge(mv_ready, along(b, lambda i: (SC + 1) * (i + 1), B - 1))
                    inverse_root(nc, pool, rstd[:], mv[:, :, 1:2], [const[:, :, k:k + 1] for k in range(3)],
                                 [work[:, :, k:k + 1] for k in range(3)], newton,
                                 along(b, lambda i: 2 * NEWTON_OPS * i, B - 1), rstd_ready)
                    pool.wait_ge(x_mv_ready, along(b, lambda i: i + 1, B - 1))
                    inverse_root(nc, pool, x_rstd[:], x_mv[:, :, 1:2], [const[:, 0:1, k:k + 1] for k in range(3)],
                                 [x_work[:, :, k:k + 1] for k in range(3)], newton,
                                 along(b, lambda i: NEWTON_OPS * (2 * i + 1), B - 1), x_rstd_ready)

                def residual(it):
                    pool.wait_ge(res_loaded, along(it, lambda i: 16 * (i + 1)))
                    if later(it):
                        pool.wait_ge(y_ready, along(it, lambda i: i))
                    nc.gpsimd.tensor_tensor(x_bo[:], x_res[:], bo_rows[0:NQ, :], ALU.add).then_inc(x_bo_ready, 1)

                roots(0)
                roots(1)
                roots(2)
                residual(0)
                with pool.Fori(1, LOOPED) as it:
                    roots(it + 2)
                    residual(it)
                residual(LOOPED)
                residual(LOOPED + 1)

            @block.tensor
            def _(pe):
                def open_unit(it, unit):
                    g = place(it if isinstance(it, int) else 1, unit)
                    if g >= 3:
                        e = readers(ORDER[g - 3])[-1]
                        pe.wait_ge(emptied[e], along(it, lambda i: BEFORE[e][place(i, unit) - 2]))
                    return bank(it, unit)

                def in_three(out, terms):
                    passes = [(a, b) for sh, sl, mh, ml in terms for a, b in ((sh, mh), (sh, ml), (sl, mh))]
                    for n, (a, b) in enumerate(passes):
                        last = nc.tensor.matmul(out, a, b, start=n == 0, stop=n == len(passes) - 1)
                    return last

                def transposes(it, unit, b):
                    ps = open_unit(it, unit)
                    if unit == "Xx":
                        pe.wait_ge(x_normed2, along(b, lambda i: i + 1, B - 1))
                        for k in range(KC):
                            last = nc.tensor.transpose(ps[:, k * NQ:(k + 1) * NQ], x_n2[:, k * P:(k + 1) * P],
                                                       ident[0:NQ, 0:NQ])
                    else:
                        k = int(unit[1])
                        pe.wait_ge(ctx_normed, along(b, lambda i: SC * (i + 1), B - 1))
                        for c in range(SC):
                            last = nc.tensor.transpose(ps[:, c * SP_:(c + 1) * SP_], ctx_n[:, c, k * P:(k + 1) * P],
                                                       ident[0:SP_, 0:SP_])
                    last.then_inc(unit_ready, 1)

                def project_k(it, m):
                    ps = open_unit(it, "K%d" % m)
                    if m == 0:
                        wait_emptied(pe, it, "X1", "D", back=1)
                    w = slice(m * P, (m + 1) * P)
                    in_three(ps[:, 0:SKE], [(wkv_hi[:, k, w], wkv_lo[:, k, w], ctxT_hi[:, k, :], ctxT_lo[:, k, :])
                                            for k in range(KC)]).then_inc(unit_ready, 1)

                def project_v(it, half):
                    w = slice(INNER + half * 512, INNER + (half + 1) * 512)
                    for c in range(SC):
                        ps = open_unit(it, "V%d%d" % (half, c))
                        s = slice(c * SP_, (c + 1) * SP_)
                        in_three(ps[0:SP_, :], [(ctxT_hi[:, k, s], ctxT_lo[:, k, s], wkv_hi[:, k, w], wkv_lo[:, k, w])
                                                for k in range(KC)]).then_inc(unit_ready, 1)

                def project_q(it, u):
                    ps = open_unit(it, "Q%d" % u)
                    if u == 0:
                        wait_emptied(pe, it, "Xx", "A", back=1)
                    for n in range(4):
                        m = 4 * u + n
                        for k in range(KC):
                            last = nc.tensor.matmul(ps[:, n * NQ:(n + 1) * NQ], wq[:, k, m * P:(m + 1) * P], xT[:, k, :],
                                                    start=k == 0, stop=k == KC - 1)
                    last.then_inc(unit_ready, 1)

                def qk(it, j):
                    if j == 0:
                        wait_emptied(pe, it, "Q1", "D", back=1)
                    for c in range(SC):
                        if later(it) or j:
                            pe.wait_ge(exp_done, along(it, lambda i: 12 * i + 3 * j + c - 3 + 1))
                        s = slice(c * SP_, (c + 1) * SP_)
                        for n in range(2):
                            m = 2 * j + n
                            last = in_three(scores[0:SP_, c, n * 2 * NQ:(n + 1) * 2 * NQ],
                                            [(k_hi[:, m, s], k_lo[:, m, s], q_hi[:, m, :], q_lo[:, m, :])])
                        last.then_inc(scores_ready, 1)

                def pv(it, j):
                    if j == 0 or j == 2:
                        for u in (V_LOW if j == 0 else V_HIGH)[1:]:
                            wait_emptied(pe, it, u, readers(u), back=1)
                    if later(it) or j >= 2:
                        pe.wait_ge(o_normed, along(it, lambda i: 4 * i + j - 2 + 1))
                    pe.wait_ge(clipped, along(it, lambda i: 12 * i + 3 * j + SC))
                    for h in range(4):
                        for c in range(SC):
                            last = nc.tensor.matmul(mixed[0:NQ, j % 2, h * D1:(h + 1) * D1],
                                                    probs[:, j % 2, c, h * NQ:(h + 1) * NQ], v[:, c, 4 * j + h, :],
                                                    start=c == 0, stop=c == SC - 1)
                    last.then_inc(mixed_ready, 1)

                def transpose_o(it, j):
                    ps = open_unit(it, "O%d" % j)
                    pe.wait_ge(o_normed, along(it, lambda i: 4 * i + j + 1))
                    for n in range(2):
                        m = 2 * j + n
                        last = nc.tensor.transpose(ps[:, n * NQ:(n + 1) * NQ], o[:, m * P:(m + 1) * P],
                                                   ident[0:NQ, 0:NQ])
                    last.then_inc(unit_ready, 1)

                def project_o(it):
                    ps = open_unit(it, "W")
                    wait_emptied(pe, it, "O3", "D")
                    in_three(ps[0:NQ, 0:DIM], [(oT_hi[:, m, :], oT_lo[:, m, :], wo_hi[:, m, :], wo_lo[:, m, :])
                                               for m in range(PAIRS)]).then_inc(unit_ready, 1)

                def iteration(it, project=True, transpose=True):
                    for j in range(QUADS):
                        qk(it, j)
                        if project:
                            project_k(it, 2 * j)
                            project_k(it, 2 * j + 1)
                        if j:
                            transpose_o(it, j - 1)
                        pv(it, j)
                        if project and j == 1:
                            project_v(it, 0)
                    if project:
                        project_q(it, 0)
                        project_q(it, 1)
                        project_v(it, 1)
                    if transpose:
                        for u in X_UNITS:
                            transposes(it, u, it + 2)
                    transpose_o(it, 3)
                    project_o(it)

                for u in X_UNITS:
                    transposes(-2, u, 0)
                for m in range(PAIRS):
                    project_k(-1, m)
                project_q(-1, 0)
                project_q(-1, 1)
                project_v(-1, 0)
                project_v(-1, 1)
                for u in X_UNITS:
                    transposes(-1, u, 1)
                iteration(0)
                with pe.Fori(1, LOOPED) as it:
                    iteration(it)
                iteration(LOOPED, transpose=False)
                iteration(LOOPED + 1, project=False, transpose=False)

            @block.scalar
            def _(act):
                def empty_x(it, unit):
                    wait_unit(act, it, unit)
                    ps = bank(it, unit)
                    if unit == "Xx":
                        for k in range(KC):
                            last = nc.scalar.activation(xT[:, k, :], ps[:, k * NQ:(k + 1) * NQ], ACT.Identity,
                                                        scale=lnl_w[:, k:k + 1], bias=lnl_b[:, k:k + 1])
                    else:
                        k = int(unit[1])
                        last = nc.scalar.activation(ctx_f[:, k, :], ps[:, 0:SK], ACT.Identity,
                                                    scale=lnc_w[:, k:k + 1], bias=lnc_b[:, k:k + 1])
                    last.then_inc(act_emptied, 1)

                def empty_k(it, m):
                    wait_unit(act, it, "K%d" % m)
                    nc.scalar.copy(k_hi[:, m, :], bank(it, "K%d" % m)[:, 0:SK]).then_inc(act_emptied, 1)

                def empty_v(it, half):
                    for c in range(SC):
                        u = "V%d%d" % (half, c)
                        if readers(u) == "A":
                            wait_unit(act, it, u)
                            nc.scalar.copy(v[:, c, 8 * half:8 * half + 8, 0:D],
                                           bank(it, u)[0:SP_, :].rearrange("p (h d) -> p h d", d=D)
                                           ).then_inc(act_emptied, 1)

                def empty_q(it, u):
                    wait_unit(act, it, "Q%d" % u)
                    ps = bank(it, "Q%d" % u)[:, 0:4 * NQ].rearrange("p (m n) -> p m n", n=NQ)
                    for e in range(2):
                        r = slice(e * D, (e + 1) * D)
                        last = nc.scalar.copy(q_hi[r, 4 * u:4 * u + 4, e * NQ:(e + 1) * NQ], ps[r])
                    last.then_inc(act_emptied, 1)

                def empty_o(it, j):
                    wait_unit(act, it, "O%d" % j)
                    nc.scalar.copy(oT_hi[:, 2 * j:2 * j + 2, :],
                                   bank(it, "O%d" % j)[:, 0:2 * NQ].rearrange("p (m n) -> p m n", n=NQ)
                                   ).then_inc(act_emptied, 1)

                def exps(it, j):
                    for c in range(SC):
                        act.wait_ge(scores_ready, along(it, lambda i: 12 * i + 3 * j + c + 1))
                        nc.scalar.activation(probs[:, j % 2, c, :], scores[0:SP_, c, 0:4 * NQ], ACT.Exp
                                             ).then_inc(exp_done, 1)

                def load_residual(it):
                    if later(it):
                        act.wait_ge(x_bo_ready, along(it, lambda i: i))
                    act.dma_start(x_res[:], io["x"][it]).then_inc(res_loaded, 16)

                def store(it):
                    act.wait_ge(y_ready, along(it, lambda i: i + 1))
                    act.dma_start(x1[it], y[:]).then_inc(stored, 16)

                def iteration(it, project=True, transpose=True):
                    load_residual(it)
                    for j in range(QUADS):
                        exps(it, j)
                        if j == 1 and later(it):
                            store(it - 1)
                        if project:
                            empty_k(it, 2 * j)
                            empty_k(it, 2 * j + 1)
                        if j:
                            empty_o(it, j - 1)
                        if project and j == 1:
                            empty_v(it, 0)
                    if project:
                        empty_q(it, 0)
                        empty_q(it, 1)
                        empty_v(it, 1)
                    if transpose:
                        for u in X_UNITS:
                            empty_x(it, u)
                    empty_o(it, 3)

                for u in X_UNITS:
                    empty_x(-2, u)
                for m in range(PAIRS):
                    empty_k(-1, m)
                empty_q(-1, 0)
                empty_q(-1, 1)
                empty_v(-1, 0)
                empty_v(-1, 1)
                for u in X_UNITS:
                    empty_x(-1, u)
                iteration(0)
                with act.Fori(1, LOOPED) as it:
                    iteration(it)
                iteration(LOOPED, transpose=False)
                iteration(LOOPED + 1, project=False, transpose=False)
                store(LOOPED + 1)
                act.wait_ge(stored, 16 * B)

            @block.vector
            def _(dve):
                def take_stats(b):
                    n = lambda k: along(b, lambda i: (SC + 1) * i + k, B - 1)
                    dve.wait_ge(ctx_loaded, along(b, lambda i: 16 * (i + 1), B - 1))
                    dve.wait_ge(x_loaded, along(b, lambda i: 16 * (i + 1), B - 1))
                    for c in range(SC):
                        nc.vector.bn_stats(stats[0:SP_, c, :], ctx_in[:, c, :]).then_inc(stats_done, 1)
                    nc.vector.bn_stats(stats[0:NQ, SC, :], x_in[:]).then_inc(stats_done, 1)
                    dve.wait_ge(stats_done, n(SC + 1))
                    nc.vector.memset(idle[:], 0.0)
                    for c in range(SC + 1):
                        r = SP_ if c < SC else NQ
                        nc.vector.bn_aggr(mv[0:r, c, :], stats[0:r, c, :]).then_inc(mv_ready, 1)

                def normalise(b, it):
                    one = along(b, lambda i: i + 1, B - 1)
                    dve.wait_ge(rstd_ready, one)
                    nc.vector.tensor_scalar(x_n1[:], x_in[:], mv[0:NQ, SC, 0:1], rstd[0:NQ, SC, :], ALU.subtract,
                                            ALU.mult).then_inc(x_normed1, 1)
                    dve.wait_ge(x_normed1, one)
                    nc.vector.bn_stats(x_stats[0:NQ, :], x_n1[:]).then_inc(x_stats_done, 1)
                    dve.wait_ge(x_stats_done, one)
                    nc.vector.memset(idle[:], 0.0)
                    nc.vector.bn_aggr(x_mv[0:NQ, 0, :], x_stats[0:NQ, :]).then_inc(x_mv_ready, 1)
                    if not isinstance(it, int) or it > -2:
                        wait_unit(dve, it, "X1", back=1)
                    for c in range(SC):
                        nc.vector.tensor_scalar(ctx_n[:, c, :], ctx_in[:, c, :], mv[0:SP_, c, 0:1], rstd[0:SP_, c, :],
                                                ALU.subtract, ALU.mult).then_inc(ctx_normed, 1)

                def normalise_x_again(b):
                    dve.wait_ge(x_rstd_ready, along(b, lambda i: i + 1, B - 1))
                    nc.vector.tensor_scalar(x_n2[:], x_n1[:], x_mv[0:NQ, 0, 0:1], x_rstd[0:NQ, 0, :], ALU.subtract,
                                            ALU.mult).then_inc(x_normed2, 1)

                def split_x(it):
                    for k in range(KC):
                        wait_emptied(dve, it, "X%d" % k, "A")
                        nc.vector.tensor_copy(ctxT_hi[:, k, 0:SK], ctx_f[:, k, :]).then_inc(head_done, 1)
                        dve.wait_ge(head_done, along(it, lambda i: KC * (i + 2) + k + 1))
                        nc.vector.tensor_tensor(ctxT_lo[:, k, 0:SK], ctx_f[:, k, :], ctxT_hi[:, k, 0:SK],
                                                ALU.subtract).then_inc(dve_emptied, 1)

                def tail_k(it, m):
                    u = "K%d" % m
                    wait_emptied(dve, it, u, "A")
                    nc.vector.tensor_tensor(k_lo[:, m, :], bank(it, u)[:, 0:SK], k_hi[:, m, :],
                                            ALU.subtract).then_inc(dve_emptied, 1)

                def empty_v(it, half):
                    for c in range(SC):
                        u = "V%d%d" % (half, c)
                        if readers(u) == "D":
                            wait_unit(dve, it, u)
                            nc.vector.tensor_copy(v[:, c, 8 * half:8 * half + 8, 0:D],
                                                  bank(it, u)[0:SP_, :].rearrange("p (h d) -> p h d", d=D)
                                                  ).then_inc(dve_emptied, 1)

                def tail_q(it, n):
                    u = "Q%d" % n
                    wait_emptied(dve, it, u, "A")
                    ps = bank(it, u)[:, 0:4 * NQ].rearrange("p (m n) -> p m n", n=NQ)
                    for e in range(2):
                        r = slice(e * D, (e + 1) * D)
                        s = (r, slice(4 * n, 4 * n + 4), slice(e * NQ, (e + 1) * NQ))
                        last = nc.vector.tensor_tensor(q_lo[s], ps[r], q_hi[s], ALU.subtract)
                    last.then_inc(dve_emptied, 1)

                def tail_o(it, j):
                    u = "O%d" % j
                    wait_emptied(dve, it, u, "A")
                    ps = bank(it, u)[:, 0:2 * NQ].rearrange("p (m n) -> p m n", n=NQ)
                    nc.vector.tensor_tensor(oT_lo[:, 2 * j:2 * j + 2, :], ps, oT_hi[:, 2 * j:2 * j + 2, :],
                                            ALU.subtract).then_inc(dve_emptied, 1)

                def clip(it, j):
                    for c in range(SC):
                        dve.wait_ge(exp_done, along(it, lambda i: 12 * i + 3 * j + c + 1))
                        nc.vector.tensor_scalar(probs[:, j % 2, c, :], probs[:, j % 2, c, :], float(np.exp(-CLIP)),
                                                float(np.exp(CLIP)), ALU.max, ALU.min).then_inc(clipped, 1)

                def norm_o(it, j):
                    q = along(it, lambda i: 4 * i + j + 1)
                    dve.wait_ge(mixed_ready, q)
                    ps = mixed[0:NQ, j % 2, 0:4 * D1].rearrange("p (h d) -> p h d", d=D1)
                    nc.vector.reciprocal(rden[:], ps[:, :, D:D1]).then_inc(rden_ready, 1)
                    dve.wait_ge(rden_ready, q)
                    nc.vector.tensor_tensor(o[:, 4 * j * D:4 * (j + 1) * D].rearrange("p (h d) -> p h d", d=D),
                                            ps[:, :, 0:D], rden[:].to_broadcast([NQ, 4, D]), ALU.mult
                                            ).then_inc(o_normed, 1)

                def finish(it):
                    wait_unit(dve, it, "W")
                    dve.wait_ge(x_bo_ready, along(it, lambda i: i + 1))
                    if later(it):
                        dve.wait_ge(stored, along(it, lambda i: 16 * i))
                    nc.vector.tensor_tensor(y[:], bank(it, "W")[0:NQ, 0:DIM], x_bo[:], ALU.add).then_inc(y_ready, 1)

                def iteration(it, project=True, transpose=True):
                    for j in range(QUADS):
                        clip(it, j)
                        if project:
                            tail_k(it, 2 * j)
                            tail_k(it, 2 * j + 1)
                        if j:
                            tail_o(it, j - 1)
                        if transpose:
                            if j == 0:
                                take_stats(it + 2)
                            if j == 1:
                                normalise(it + 2, it)
                            if j == 2:
                                normalise_x_again(it + 2)
                        norm_o(it, j)
                        if project and j == 1:
                            empty_v(it, 0)
                    if project:
                        tail_q(it, 0)
                        tail_q(it, 1)
                        empty_v(it, 1)
                    if transpose:
                        split_x(it)
                    tail_o(it, 3)
                    finish(it)

                take_stats(0)
                normalise(0, -2)
                normalise_x_again(0)
                split_x(-2)
                take_stats(1)
                normalise(1, -1)
                normalise_x_again(1)
                for m in range(PAIRS):
                    tail_k(-1, m)
                tail_q(-1, 0)
                tail_q(-1, 1)
                empty_v(-1, 0)
                empty_v(-1, 1)
                split_x(-1)
                iteration(0)
                with dve.Fori(1, LOOPED) as it:
                    iteration(it)
                iteration(LOOPED, transpose=False)
                iteration(LOOPED + 1, project=False, transpose=False)


T_UNITS = ["T%d" % r for r in range(RS)]
F_TILE = ([g + str(m) for m in range(HC) for g in "GH"] + ["M%d" % m for m in range(HC)]
          + ["N%d" % m for m in range(HC)] + T_UNITS + ["F%d" % r for r in range(RS)])
F_LAST = [u for u in F_TILE if u not in T_UNITS]
F_ORDER = T_UNITS + F_TILE * (TILES - 1) + F_LAST
F_BEFORE = {e: prefix(F_ORDER, e, lambda u: "D" if u[0] in "HF" else "A") for e in "AD"}


def f_place(t, unit):
    if t == -1:
        return T_UNITS.index(unit)
    return len(T_UNITS) + len(F_TILE) * t + (F_TILE if t < TILES - 1 else F_LAST).index(unit)


def feed_forward(nc, io, x1, out):
    with ExitStack() as ctx:
        def sb(name, shape, dt=F32):
            return ctx.enter_context(nc.sbuf_tensor(name, shape, dt))

        def sem(name):
            return ctx.enter_context(nc.semaphore(name))

        w1 = sb("w1", [P, KC, HID])
        w2 = sb("w2", [P, KC, HID])
        h1 = sb("h1", [P, HC, HID])
        h2 = sb("h2", [P, HC, HID])
        w3 = sb("w3", [P, HC, DIM])
        s1 = sb("s1", [P, HC])
        s2 = sb("s2", [P, HC])
        t1 = sb("t1", [P, HC])
        t2 = sb("t2", [P, HC])
        s3_rows = sb("s3_rows", [P, DIM])
        ident = sb("f_ident", [P, P])
        x_in = sb("f_x_in", [P, RS, DIM])
        x_res = sb("f_x_res", [P, RS, DIM])
        x_n = sb("f_x_n", [P, RS, DIM])
        stats = sb("f_stats", [P, RS, 6])
        mv = sb("f_mv", [P, RS, 2])
        rstd = sb("f_rstd", [P, RS, 1])
        const = sb("f_const", [P, RS, 3])
        work = sb("f_work", [P, RS, 3])
        idle = sb("f_idle", [P, 1])
        xT = sb("f_xT", [P, KC, TR])
        gate = sb("gate", [P, 2, TR])
        act_a = sb("act_a", [P, HC, TR])
        act_b = sb("act_b", [P, HC, TR])
        y = sb("f_y", [P, RS, DIM])
        banks = ctx.enter_context(nc.psum_tensor("banks", [P, 8, 512], F32))

        w_in = {n: sem("in_" + n) for n in ("w1", "w2", "h1", "h2", "w3")}
        small_in, s3_in, f_ident_set = sem("f_small_in"), sem("s3_in"), sem("f_ident_set")
        f_const_set = sem("f_const_set")
        x_loaded, res_loaded = sem("f_x_loaded"), sem("f_res_loaded")
        stats_done, mv_ready, rstd_ready, x_normed = sem("f_stats_done"), sem("f_mv_ready"), sem("f_rstd_ready"), sem("f_x_normed")
        newton = sem("f_newton")
        unit_ready, act_emptied, dve_emptied = sem("f_unit_ready"), sem("f_act_emptied"), sem("f_dve_emptied")
        scaled, summed, stored = sem("f_scaled"), sem("f_summed"), sem("f_stored")
        emptied = {"A": act_emptied, "D": dve_emptied}
        x_tiles = x1.rearrange("b n d -> (b n) d").rearrange("(t r p) d -> t p r d", r=RS, p=P)
        out_tiles = out.rearrange("b n d -> (b n) d").rearrange("(t r p) d -> t p r d", r=RS, p=P)

        def over(t, f):
            return along(t, f, TILES - 2)

        def bank(t, unit):
            return banks[:, f_place(t if isinstance(t, int) else 1, unit) % 8, :]

        def wait_unit(eng, t, unit):
            eng.wait_ge(unit_ready, over(t, lambda i: f_place(i, unit) + 1))

        def wait_emptied(eng, t, unit, engine, back=0):
            eng.wait_ge(emptied[engine], over(t, lambda i: F_BEFORE[engine][f_place(i - back, unit) + 1]))

        with nc.Block() as block:
            @block.sync
            def _(sp):
                def load(t):
                    if later(t):
                        sp.wait_ge(x_normed, over(t, lambda i: RS * i))
                    sp.dma_start(x_in[:], x_tiles[t]).then_inc(x_loaded, 16)

                load(0)
                for n, w in (("w1", w1), ("w2", w2), ("h1", h1), ("h2", h2), ("w3", w3)):
                    sp.dma_start(w[:], io[n]).then_inc(w_in[n], 16)
                sp.dma_start(x_res[:], x_tiles[0]).then_inc(res_loaded, 16)
                load(1)
                with sp.Fori(1, TILES - 1) as t:
                    load(t + 1)
                    sp.wait_ge(summed, over(t, lambda i: RS * i))
                    sp.dma_start(x_res[:], x_tiles[t]).then_inc(res_loaded, 16)
                sp.wait_ge(summed, RS * (TILES - 1))
                sp.dma_start(x_res[:], x_tiles[TILES - 1]).then_inc(res_loaded, 16)

            @block.gpsimd
            def _(pool):
                def roots(t):
                    pool.wait_ge(mv_ready, along(t, lambda i: RS * (i + 1), TILES - 1))
                    inverse_root(nc, pool, rstd[:], mv[:, :, 1:2], [const[:, :, k:k + 1] for k in range(3)],
                                 [work[:, :, k:k + 1] for k in range(3)], newton,
                                 along(t, lambda i: NEWTON_OPS * i, TILES - 1), rstd_ready)

                for k, c in enumerate((EPS, -0.5, 1.5)):
                    nc.gpsimd.memset(const[:, :, k:k + 1], c).then_inc(f_const_set, 1)
                nc.gpsimd.memset(ident[:], 0.0).then_inc(f_ident_set, 1)
                pool.wait_ge(f_ident_set, 1)
                nc.gpsimd.affine_select(out=ident[:], in_=ident[:], compare_op=ALU.not_equal, fill=1.0,
                                        base=0, pattern=[[-1, P]], channel_multiplier=1).then_inc(f_ident_set, 1)
                pool.wait_ge(f_const_set, 3)
                roots(0)
                with pool.Fori(1, TILES) as t:
                    roots(t)

            @block.tensor
            def _(pe):
                def open_unit(t, unit):
                    g = f_place(t if isinstance(t, int) else 1, unit)
                    if g >= 8:
                        e = "D" if F_ORDER[g - 8][0] in "HF" else "A"
                        pe.wait_ge(emptied[e], over(t, lambda i: F_BEFORE[e][f_place(i, unit) - 7]))
                    return bank(t, unit)

                def transposes(t, r):
                    ps = open_unit(t, "T%d" % r)
                    pe.wait_ge(x_normed, over(t, lambda i: RS * (i + 1) + r + 1))
                    for k in range(KC):
                        last = nc.tensor.transpose(ps[:, k * P:(k + 1) * P], x_n[:, r, k * P:(k + 1) * P], ident[:])
                    last.then_inc(unit_ready, 1)

                def glu(t, m):
                    if m == 0:
                        wait_emptied(pe, t, "T%d" % (RS - 1), "A", back=1)
                    for g, w in (("G", w1), ("H", w2)):
                        ps = open_unit(t, g + str(m))
                        if m == 0 and isinstance(t, int) and t == 0:
                            pe.wait_ge(w_in["w1" if g == "G" else "w2"], 16)
                        for k in range(KC):
                            last = nc.tensor.matmul(ps, w[:, k, m * P:(m + 1) * P], xT[:, k, :], start=k == 0,
                                                    stop=k == KC - 1)
                        last.then_inc(unit_ready, 1)

                def hidden(t, m, name, w, source, before, engine):
                    ps = open_unit(t, name + str(m))
                    if m == 0 and isinstance(t, int) and t == 0:
                        pe.wait_ge(w_in["h1" if name == "M" else "h2"], 16)
                    for k in range(HC):
                        if m == 0:
                            wait_emptied(pe, t, before + str(k), engine)
                        last = nc.tensor.matmul(ps, w[:, k, m * P:(m + 1) * P], source[:, k, :], start=k == 0,
                                                stop=k == HC - 1)
                    last.then_inc(unit_ready, 1)

                def down(t, r):
                    ps = open_unit(t, "F%d" % r)
                    if r == 0:
                        wait_emptied(pe, t, "N%d" % (HC - 1), "A")
                        if isinstance(t, int) and t == 0:
                            pe.wait_ge(w_in["w3"], 16)
                    for k in range(HC):
                        last = nc.tensor.matmul(ps[:, 0:DIM], act_a[:, k, r * P:(r + 1) * P], w3[:, k, :],
                                                start=k == 0, stop=k == HC - 1)
                    last.then_inc(unit_ready, 1)

                def tile(t, more=True):
                    for m in range(HC):
                        glu(t, m)
                    for m in range(HC):
                        hidden(t, m, "M", h1, act_a, "H", "D")
                    for m in range(HC):
                        hidden(t, m, "N", h2, act_b, "M", "A")
                    if more:
                        for r in range(RS):
                            transposes(t, r)
                    for r in range(RS):
                        down(t, r)

                pe.wait_ge(f_ident_set, 2)
                for r in range(RS):
                    transposes(-1, r)
                tile(0)
                with pe.Fori(1, TILES - 1) as t:
                    tile(t)
                tile(TILES - 1, more=False)

            @block.scalar
            def _(act):
                for t, n in ((s1, "s1"), (s2, "s2"), (t1, "t1"), (t2, "t2")):
                    act.dma_start(t[:], io[n]).then_inc(small_in, 16)
                act.dma_start(s3_rows[:], io["s3"].partition_broadcast(P)).then_inc(s3_in, 16)

                def empty_t(t, r):
                    wait_unit(act, t, "T%d" % r)
                    nc.scalar.copy(xT[:, :, r * P:(r + 1) * P],
                                   bank(t, "T%d" % r)[:, 0:KC * P].rearrange("p (k n) -> p k n", n=P)
                                   ).then_inc(act_emptied, 1)

                def tile(t, more=True):
                    for m in range(HC):
                        wait_unit(act, t, "G%d" % m)
                        if later(t) or m >= 2:
                            act.wait_ge(dve_emptied, over(t, lambda i: F_BEFORE["D"][f_place(
                                i if m >= 2 else i - 1, "H%d" % ((m - 2) % HC)) + 1]))
                        nc.scalar.activation(gate[:, m % 2, :], bank(t, "G%d" % m), ACT.Silu,
                                             scale=s1[:, m:m + 1]).then_inc(act_emptied, 1)
                    for name, dst, s in (("M", act_b, t1), ("N", act_a, t2)):
                        for m in range(HC):
                            wait_unit(act, t, name + str(m))
                            nc.scalar.activation(dst[:, m, :], bank(t, name + str(m)), ACT.Gelu,
                                                 scale=s[:, m:m + 1]).then_inc(act_emptied, 1)
                    if more:
                        for r in range(RS):
                            empty_t(t, r)
                    act.wait_ge(summed, over(t, lambda i: RS * (i + 1)))
                    act.dma_start(out_tiles[t], y[:]).then_inc(stored, 16)

                for r in range(RS):
                    empty_t(-1, r)
                act.wait_ge(small_in, 64)
                tile(0)
                with act.Fori(1, TILES - 1) as t:
                    tile(t)
                tile(TILES - 1, more=False)
                act.wait_ge(stored, 16 * TILES)

            @block.vector
            def _(dve):
                def normalise(t, turn):
                    n = lambda k: along(t, lambda i: RS * i + k, TILES - 1)
                    dve.wait_ge(x_loaded, along(t, lambda i: 16 * (i + 1), TILES - 1))
                    for r in range(RS):
                        nc.vector.bn_stats(stats[:, r, :], x_in[:, r, :]).then_inc(stats_done, 1)
                    dve.wait_ge(stats_done, n(RS))
                    nc.vector.memset(idle[:], 0.0)
                    for r in range(RS):
                        nc.vector.bn_aggr(mv[:, r, :], stats[:, r, :]).then_inc(mv_ready, 1)
                    dve.wait_ge(rstd_ready, along(t, lambda i: i + 1, TILES - 1))
                    if turn is not None:
                        dve.wait_ge(unit_ready, over(turn, lambda i: f_place(i - 1, "T%d" % (RS - 1)) + 1))
                    for r in range(RS):
                        nc.vector.tensor_scalar(x_n[:, r, :], x_in[:, r, :], mv[:, r, 0:1], rstd[:, r, :],
                                                ALU.subtract, ALU.mult).then_inc(x_normed, 1)

                def tile(t, more=True):
                    for m in range(HC):
                        wait_unit(dve, t, "H%d" % m)
                        wait_emptied(dve, t, "G%d" % m, "A")
                        nc.vector.scalar_tensor_tensor(out=act_a[:, m, :], in0=bank(t, "H%d" % m), scalar=s2[:, m:m + 1],
                                                       in1=gate[:, m % 2, :], op0=ALU.mult, op1=ALU.mult
                                                       ).then_inc(dve_emptied, 1)
                    if more:
                        normalise(t + 1, t)
                    if later(t):
                        dve.wait_ge(stored, over(t, lambda i: 16 * i))
                    dve.wait_ge(res_loaded, over(t, lambda i: 16 * (i + 1)))
                    for r in range(RS):
                        wait_unit(dve, t, "F%d" % r)
                        nc.vector.tensor_tensor(y[:, r, :], bank(t, "F%d" % r)[:, 0:DIM], s3_rows[:], ALU.mult
                                                ).then_inc(dve_emptied, 1)
                        wait_emptied(dve, t, "F%d" % r, "D")
                        nc.vector.tensor_tensor(y[:, r, :], y[:, r, :], x_res[:, r, :], ALU.add).then_inc(summed, 1)

                normalise(0, None)
                dve.wait_ge(s3_in, 16)
                dve.wait_ge(small_in, 64)
                tile(0)
                with dve.Fori(1, TILES - 1) as t:
                    tile(t)
                tile(TILES - 1, more=False)


def program(nc, io, out):
    x1 = nc.dram_tensor("x1", [B, NQ, DIM], F32, kind="Internal").ap()
    attention(nc, io, x1)
    feed_forward(nc, io, x1, out)


def kernel(**inputs):
    import concourse.bacc as bacc
    from concourse.bass_utils import run_bass_kernel_spmd

    a = {k: np.asarray(w) for k, w in inputs.items()}

    def chunked(w):
        return w.reshape(-1, P, w.shape[-1]).transpose(1, 0, 2)

    x, xa, ff = "x", "L0_xattn_", "L0_ffn_"
    arrays = {
        "x": a["x"],
        "ctx": a["ctx_1024"].reshape(B, SC, SP_, DIM).transpose(0, 2, 1, 3),
        "lnl_w": a[xa + "ln_l_w"].reshape(KC, P).T, "lnl_b": a[xa + "ln_l_b"].reshape(KC, P).T,
        "lnc_w": a[xa + "ln_c_w"].reshape(KC, P).T, "lnc_b": a[xa + "ln_c_b"].reshape(KC, P).T,
        "wq": chunked(a[xa + "Wq"]), "wkv": a[xa + "Wkv"].reshape(KC, P, 2 * INNER), "wo": chunked(a[xa + "Wo"]),
        "bo": a[xa + "bo"],
        "w1": chunked(a[ff + "w1_w"].T), "w2": chunked(a[ff + "w2_w"].T),
        "h1": chunked(a[ff + "h1_w"].T), "h2": chunked(a[ff + "h2_w"].T), "w3": chunked(a[ff + "w3_w"].T),
        "s1": a[ff + "w1_s"].reshape(HC, P).T, "s2": a[ff + "w2_s"].reshape(HC, P).T,
        "t1": a[ff + "h1_s"].reshape(HC, P).T, "t2": a[ff + "h2_s"].reshape(HC, P).T,
        "s3": a[ff + "w3_s"],
    }
    nc = bacc.Bacc("TRN2", target_bir_lowering=False, num_devices=1)
    io, feeds = {}, {}
    for name, w in arrays.items():
        w = np.ascontiguousarray(w)
        feeds["in_" + name + "_dram"] = w
        io[name] = nc.dram_tensor("in_" + name + "_dram", w.shape, mybir.dt.from_np(w.dtype), kind="ExternalInput").ap()
    out = nc.dram_tensor("out_dram", [B, NQ, DIM], F32, kind="ExternalOutput").ap()
    program(nc, io, out)
    result = run_bass_kernel_spmd(nc, [feeds], core_ids=[0])
    return result.results[0]["out_dram"]
```

```python
from contextlib import ExitStack

import numpy as np

import concourse.bass as bass
from concourse import mybir

ALU = mybir.AluOpType
ACT = mybir.ActivationFunctionType
F32 = mybir.dt.float32
F32R = mybir.dt.float32r
I32 = mybir.dt.int32

B, NQ, DIM = 32, 112, 256
SK, H, D = 375, 16, 64
INNER = H * D
HID = 1024
P = 128
KC = DIM // P
SC, SP_ = 3, SK // 3
SKE = SK + 1
PAIRS = H // 2
QUADS = H // 4
D1 = D + 1
KV_PARTS = 4
KV_COLS = 2 * INNER // KV_PARTS
EPS = 1e-5
CLIP = 11.0
LOOPED = B - 2
MAGIC = 1597463007.0
NEWTON = 3

ROWS = B * NQ
TR = 512
TILES = ROWS // TR
RS = TR // P
FIRST_ENTRIES = -(-TR // NQ)
assert RS == SC + 1
HC = HID // P
W_COLS = {"w1": KC * HID, "w2": KC * HID, "h1": HC * HID, "h2": HC * HID, "w3": HC * DIM}
FF_SCALES = ["s1", "s2", "t1", "t2"]
EARLY = W_COLS["w1"] + W_COLS["w2"] + W_COLS["h1"]
PIECE = 768
EARLY_PIECES = EARLY // PIECE
PIECES = -(-sum(W_COLS.values()) // PIECE)
assert PIECES == LOOPED and EARLY % PIECE == 0
LOW_BITS = 0xFFF

X_UNITS = ["Xx", "X0", "X1"]
V_LOW = ["V00", "V01", "V02"]
V_HIGH = ["V10", "V11", "V12"]
ATTEND = ["O0", "O1", "O2", "O3", "W"]
PRO = (["X0", "X1", "K0", "K1", "Xx"] + ["K%d" % m for m in range(2, PAIRS)] + ["Q0", "Q1"] + V_LOW
       + ["V10", "Xx", "V11", "V12", "X0", "X1"])
TAIL_UNITS = ["Q0", "V10", "Q1", "Xx", "V11", "O3", "V12", "X0", "X1", "W"]
STEADY = (["K0", "K1", "K2", "K3", "O0"] + V_LOW + ["K4", "K5", "O1", "K6", "K7", "O2"] + TAIL_UNITS)
LATE = [u for u in STEADY if u not in X_UNITS]
ORDER = PRO + STEADY * LOOPED + LATE + ATTEND
READERS = {"K": "AD", "Q": "A", "O": "AD", "W": "Y", "X": "AD"}


def readers(unit):
    if unit[0] == "V":
        return "D" if unit in ("V01", "V10") else "A"
    return "A" if unit == "Xx" else READERS[unit[0]]


def prefix(order, engine, which):
    out = [0]
    for u in order:
        out.append(out[-1] + (engine in which(u)))
    return out


BEFORE = {e: prefix(ORDER, e, readers) for e in "ADY"}


def in_ring(unit):
    return unit[0] in "KQV" or unit in ("X0", "X1")


RING = [g for g, u in enumerate(ORDER) if in_ring(u)]
RING_BEFORE = [0]
for u in ORDER:
    RING_BEFORE.append(RING_BEFORE[-1] + in_ring(u))
assert sum(map(in_ring, STEADY)) % 3 == 0


def place(it, unit):
    if it == -2:
        return PRO.index(unit)
    if it == -1:
        return len(PRO) - 1 - PRO[::-1].index(unit)
    base = len(PRO) + len(STEADY) * min(it, LOOPED) + (len(LATE) if it > LOOPED else 0)
    names = STEADY if it < LOOPED else LATE if it == LOOPED else ATTEND
    return base + names.index(unit)


def along(it, f, last=LOOPED - 1):
    if isinstance(it, int):
        return f(it)
    step = f(2) - f(1)
    assert all(f(i) == f(1) + step * (i - 1) for i in range(1, last + 1))
    return it * step + (f(1) - step)


def inverse_root(nc, pool, out, var, const, work, newton, first, done):
    v, h, t = work[0], work[1], work[2]
    eps, minus_half, one_half_more = const[0], const[1], const[2]
    pool_ops = nc.gpsimd

    pool_ops.tensor_tensor(v, var, eps, ALU.add).then_inc(newton, 1)
    pool.wait_ge(newton, first + 1)
    pool_ops.tensor_tensor(h, v, minus_half, ALU.mult).then_inc(newton, 1)
    pool_ops.tensor_scalar(out.bitcast(I32), v.bitcast(I32), -0.5, MAGIC, ALU.mult, ALU.add).then_inc(newton, 1)
    for k in range(NEWTON):
        n = first + 3 + 4 * k
        pool.wait_ge(newton, n)
        pool_ops.tensor_tensor(t, out, out, ALU.mult).then_inc(newton, 1)
        pool.wait_ge(newton, n + 1)
        pool_ops.tensor_tensor(t, t, h, ALU.mult).then_inc(newton, 1)
        pool.wait_ge(newton, n + 2)
        pool_ops.tensor_tensor(t, t, one_half_more, ALU.add).then_inc(newton, 1)
        pool.wait_ge(newton, n + 3)
        last = k == NEWTON - 1
        pool_ops.tensor_tensor(out, out, t, ALU.mult).then_inc(done if last else newton, 1)


NEWTON_OPS = 3 + 4 * NEWTON - 1


def row_tiles(rows):
    return rows.rearrange("b n d -> (b n) d").rearrange("(t r p) d -> t p r d", r=RS, p=P)


def later(it):
    return not isinstance(it, int) or it > 0


def tail_units(project, transpose):
    return [u for u in TAIL_UNITS if (u[0] not in "QV" or project) and (u[0] != "X" or transpose)]


def in_pieces(tile):
    return tile.rearrange("p (n c) -> p n c", c=PIECE)


def attention(nc, io, x1, ff_copy, outlast):
    with ExitStack() as ctx:
        def sb(name, shape, dt=F32):
            return ctx.enter_context(nc.sbuf_tensor(name, shape, dt))

        def sem(name):
            return ctx.enter_context(nc.semaphore(name))

        wkv_hi = sb("wkv_hi", [P, KC, 2 * INNER], F32R)
        wkv_lo = sb("wkv_lo", [P, KC, 2 * INNER], F32R)
        wq = sb("wq", [P, KC, INNER])
        wo_hi = sb("wo_hi", [P, PAIRS, DIM], F32R)
        wo_lo = sb("wo_lo", [P, PAIRS, DIM], F32R)
        lnl_w = sb("lnl_w", [P, KC])
        lnl_b = sb("lnl_b", [P, KC])
        lnc_w = sb("lnc_w", [P, KC])
        lnc_b = sb("lnc_b", [P, KC])
        bo_rows = sb("bo_rows", [P, DIM])
        ctx_in = sb("ctx_in", [SP_, SC, DIM])
        x_in = sb("x_in", [NQ, DIM])
        stats = sb("stats", [P, SC + 1, 6])
        mv = sb("mv", [P, SC + 1, 2])
        x_stats = sb("x_stats", [P, 6])
        x_mv = sb("x_mv", [P, 1, 2])
        rstd = sb("rstd", [P, SC + 1, 1])
        x_rstd = sb("x_rstd", [P, 1, 1])
        const = sb("newton_const", [P, SC + 1, 3])
        work = sb("newton_work", [P, SC + 1, 3])
        x_work = sb("newton_x_work", [P, 1, 3])
        idle = sb("idle", [P, 1])
        ctx_n = sb("ctx_n", [SP_, SC, DIM])
        x_n1 = sb("x_n1", [NQ, DIM])
        x_n2 = sb("x_n2", [NQ, DIM])
        ctx_f = sb("ctx_f", [P, KC, SK])
        ctxT_hi = sb("ctxT_hi", [P, KC, SKE], F32R)
        ctxT_lo = sb("ctxT_lo", [P, KC, SKE], F32R)
        xT = sb("xT", [P, KC, NQ])
        k_hi = sb("k_hi", [P, PAIRS, SK], F32R)
        k_lo = sb("k_lo", [P, PAIRS, SK], F32R)
        q_hi = sb("q_hi", [P, PAIRS, 2 * NQ], F32R)
        q_lo = sb("q_lo", [P, PAIRS, 2 * NQ], F32R)
        q_full = sb("q_full", [P, 4 * NQ])
        v = sb("v", [SP_, SC, H, D1])
        probs = sb("probs", [SP_, 2, SC, 4 * NQ])
        rden = sb("rden", [NQ, 4, 1])
        o = sb("o", [NQ, INNER])
        oT_hi = sb("oT_hi", [P, PAIRS, NQ], F32R)
        oT_lo = sb("oT_lo", [P, PAIRS, NQ], F32R)
        x_res = sb("x_res", [NQ, DIM])
        piece_low = sb("piece_low", [P, 1])

        def kept(name, shape):
            return outlast.enter_context(nc.sbuf_tensor(name, shape, F32, side="right"))

        low_seen = kept("low_seen", [P, 1])
        y = kept("y", [P, DIM])[0:NQ, :]
        ones = kept("ones", [P, 1])
        ident = kept("ident", [P, P])
        ff_scales = [kept(name, [P, HC]) for name in FF_SCALES]
        with ExitStack() as before:
            piece = before.enter_context(nc.sbuf_tensor("piece", [P, PIECE], I32, side="right"))
            low_bits = before.enter_context(nc.sbuf_tensor("low_bits", [P, PIECE], I32, side="right"))
        assert RS * DIM <= 2 * PIECE
        first_rows = kept("first_rows", [P, 2 * PIECE])[:, 0:RS * DIM].rearrange("p (r d) -> p r d", r=RS)

        with ExitStack() as before:
            raw_kv = before.enter_context(nc.sbuf_tensor("raw_kv", [P, KC, 2 * INNER], F32, side="right"))
            raw_o = before.enter_context(nc.sbuf_tensor("raw_o", [P, PAIRS, DIM], F32, side="right"))
        early = kept("ff_early", [P, EARLY])
        shared = ctx.enter_context(nc.psum_tensor("shared", [P, 3, 512], F32))
        scores = ctx.enter_context(nc.psum_tensor("scores", [P, 3, 512], F32))
        mixed = ctx.enter_context(nc.psum_tensor("mixed", [P, 2, 512], F32))

        kv_in = [sem("kv_in%d" % n) for n in range(KV_PARTS)]
        wo_in, wq_in, bo_in, small_in, scaled = sem("wo_in"), sem("wq_in"), sem("bo_in"), sem("small_in"), sem("scaled")
        wo_cut = sem("wo_cut")
        heads, tails, ones_set, ident_set = sem("heads"), sem("tails"), sem("ones_set"), sem("ident_set")
        zeros_set = sem("zeros_set")
        ctx_loaded, x_loaded = sem("ctx_loaded"), sem("x_loaded")
        stats_done, mv_ready, rstd_ready = sem("stats_done"), sem("mv_ready"), sem("rstd_ready")
        x_normed1, x_stats_done, x_mv_ready = sem("x_normed1"), sem("x_stats_done"), sem("x_mv_ready")
        x_rstd_ready, x_normed2, ctx_normed = sem("x_rstd_ready"), sem("x_normed2"), sem("ctx_normed")
        newton = sem("newton")
        unit_ready = sem("unit_ready")
        act_emptied = sem("act_emptied")
        dve_emptied = sem("dve_emptied")
        head_done, q_heads, q_ready = sem("head_done"), sem("q_heads"), sem("q_ready")
        scores_ready, exp_done, clipped = sem("scores_ready"), sem("exp_done"), sem("clipped")
        mixed_ready, rden_ready, o_normed = sem("mixed_ready"), sem("rden_ready"), sem("o_normed")
        piece_in, piece_masked, piece_out = sem("piece_in"), sem("piece_masked"), sem("piece_out")
        piece_reduced, piece_seen = sem("piece_reduced"), sem("piece_seen")
        scales_in = sem("scales_in")
        early_in, rows_in, rows_normed = sem("early_in"), sem("rows_in"), sem("rows_normed")
        res_loaded, residual_ready, y_ready = sem("res_loaded"), sem("residual_ready"), sem("y_ready")
        stored = outlast.enter_context(nc.semaphore("stored"))
        emptied = {"A": act_emptied, "D": dve_emptied, "Y": y_ready}

        def wait_emptied(eng, it, unit, engine, back=0):
            eng.wait_ge(emptied[engine], along(it, lambda i: BEFORE[engine][place(i - back, unit) + 1]))

        def bank(it, unit):
            if in_ring(unit):
                return shared[:, RING_BEFORE[place(it if isinstance(it, int) else 1, unit)] % 3, :]
            if unit == "W":
                return mixed[:, 0, :]
            return mixed[:, 0 if unit == "Xx" else int(unit[1]) % 2, 4 * D1:]

        def wait_unit(eng, it, unit, back=0):
            eng.wait_ge(unit_ready, along(it, lambda i: place(i - back, unit) + 1))

        with nc.Block() as block:
            @block.sync
            def _(sp):
                def load(b):
                    sp.wait_ge(ctx_normed, b * SC)
                    sp.dma_start(ctx_in[:], io["ctx"][b]).then_inc(ctx_loaded, 16)
                    sp.wait_ge(x_normed1, b)
                    sp.dma_start(x_in[:], io["x"][b]).then_inc(x_loaded, 16)

                sp.dma_start(ctx_in[:], io["ctx"][0]).then_inc(ctx_loaded, 16)
                sp.dma_start(x_in[:], io["x"][0]).then_inc(x_loaded, 16)
                for n in range(KV_PARTS):
                    w = slice(n * KV_COLS, (n + 1) * KV_COLS)
                    sp.dma_start(raw_kv[:, :, w], io["wkv"].rearrange("k p n -> p k n")[:, :, w]
                                 ).then_inc(kv_in[n], 16)
                    if n == 1:
                        sp.dma_start(wq[:], io["wq"]).then_inc(wq_in, 16)
                        load(1)
                sp.dma_start(raw_o[:], io["wo"]).then_inc(wo_in, 16)
                sp.dma_start(bo_rows[:], io["bo"].partition_broadcast(P)).then_inc(bo_in, 16)
                for t, name in zip(ff_scales, FF_SCALES):
                    sp.dma_start(t[:], io[name]).then_inc(scales_in, 16)

                def copy_piece(n):
                    if later(n):
                        sp.wait_ge(piece_out, n * 16)
                        sp.wait_ge(piece_masked, n)
                    sp.dma_start(piece[:], io["ff"][n].bitcast(I32)).then_inc(piece_in, 16)
                    sp.wait_ge(piece_in, n * 16 + 16)
                    sp.dma_start(ff_copy[n].bitcast(I32), piece[:]).then_inc(piece_out, 16)

                load(2)
                copy_piece(0)
                with sp.Fori(1, PIECES) as n:
                    load(n + 2)
                    copy_piece(n)
                sp.wait_ge(stored, 16 * FIRST_ENTRIES)
                sp.wait_ge(piece_out, 16 * PIECES)
                sp.wait_ge(piece_reduced, PIECES)
                sp.dma_start(first_rows, row_tiles(x1)[0]).then_inc(rows_in, 16)
                sp.wait_ge(tails, KV_PARTS)
                sp.wait_ge(wo_cut, 1)
                sp.dma_start(in_pieces(early[:]), ff_copy[0:EARLY_PIECES].rearrange("n p c -> p n c")).then_inc(early_in, 16)
                sp.wait_ge(early_in, 16)
                sp.wait_ge(scales_in, 16 * len(FF_SCALES))

            @block.gpsimd
            def _(pool):
                def roots(b):
                    pool.wait_ge(mv_ready, along(b, lambda i: (SC + 1) * (i + 1), B - 1))
                    inverse_root(nc, pool, rstd[:], mv[:, :, 1:2], [const[:, :, k:k + 1] for k in range(3)],
                                 [work[:, :, k:k + 1] for k in range(3)], newton,
                                 along(b, lambda i: 2 * NEWTON_OPS * i, B - 1), rstd_ready)
                    pool.wait_ge(x_mv_ready, along(b, lambda i: i + 1, B - 1))
                    inverse_root(nc, pool, x_rstd[:], x_mv[:, :, 1:2], [const[:, 0:1, k:k + 1] for k in range(3)],
                                 [x_work[:, :, k:k + 1] for k in range(3)], newton,
                                 along(b, lambda i: NEWTON_OPS * (2 * i + 1), B - 1), x_rstd_ready)

                def residual(it):
                    pool.wait_ge(res_loaded, along(it, lambda i: 16 * (i + 1)))
                    nc.gpsimd.tensor_tensor(x_res[:], x_res[:], bo_rows[0:NQ, :], ALU.add).then_inc(residual_ready, 1)

                nc.gpsimd.memset(ident[:], 0.0).then_inc(ident_set, 1)
                pool.wait_ge(ident_set, 1)
                nc.gpsimd.affine_select(out=ident[:], in_=ident[:], compare_op=ALU.not_equal, fill=1.0,
                                        base=0, pattern=[[-1, P]], channel_multiplier=1).then_inc(ident_set, 1)
                nc.gpsimd.memset(ones[:], 1.0).then_inc(ident_set, 1)
                nc.gpsimd.memset(v[:, :, :, D:D1], 1.0).then_inc(zeros_set, 1)
                for t in (ctxT_hi, ctxT_lo):
                    nc.gpsimd.memset(t[:, :, SK:SKE].bitcast(F32), 0.0).then_inc(zeros_set, 1)
                pool.wait_ge(ones_set, 6)
                roots(0)
                for t in (q_hi, q_lo):
                    nc.gpsimd.memset(t[:].bitcast(F32), 0.0).then_inc(zeros_set, 1)
                roots(1)
                pool.wait_ge(heads, KV_PARTS + 1)
                nc.gpsimd.tensor_tensor(wo_lo[:], raw_o[:], wo_hi[:], ALU.subtract).then_inc(wo_cut, 1)
                roots(2)
                pool.wait_ge(bo_in, 16)
                residual(0)
                with pool.Fori(1, LOOPED) as it:
                    roots(it + 2)
                    residual(it)
                residual(LOOPED)
                pool.wait_ge(mv_ready, (SC + 1) * (B + 1))
                inverse_root(nc, pool, rstd[:], mv[:, :, 1:2], [const[:, :, k:k + 1] for k in range(3)],
                             [work[:, :, k:k + 1] for k in range(3)], newton, 2 * NEWTON_OPS * B, rstd_ready)
                residual(LOOPED + 1)

            @block.tensor
            def _(pe):
                def open_unit(it, unit):
                    n = RING_BEFORE[place(it if isinstance(it, int) else 1, unit)]
                    if in_ring(unit) and n >= 3:
                        e = readers(ORDER[RING[n - 3]])[-1]
                        pe.wait_ge(emptied[e], along(it, lambda i: BEFORE[e][RING[RING_BEFORE[place(i, unit)] - 3] + 1]))
                    return bank(it, unit)

                def in_three(out, terms, start=True, stop=True):
                    passes = [(a, b) for sh, sl, mh, ml in terms for a, b in ((sh, mh), (sh, ml), (sl, mh))]
                    for n, (a, b) in enumerate(passes):
                        last = nc.tensor.matmul(out, a, b, start=start and n == 0,
                                                stop=stop and n == len(passes) - 1)
                    return last

                def transposes(it, unit, b):
                    ps = open_unit(it, unit)
                    if unit == "Xx":
                        if not isinstance(it, int) or it >= 0:
                            wait_emptied(pe, it, "O2", "D")
                        elif it == -1:
                            wait_emptied(pe, it, "Xx", "A", back=1)
                        pe.wait_ge(x_normed2, along(b, lambda i: i + 1, B - 1))
                        for k in range(KC):
                            last = nc.tensor.transpose(ps[:, k * NQ:(k + 1) * NQ], x_n2[:, k * P:(k + 1) * P],
                                                       ident[0:NQ, 0:NQ])
                    else:
                        k = int(unit[1])
                        pe.wait_ge(ctx_normed, along(b, lambda i: SC * (i + 1), B - 1))
                        for c in range(SC):
                            last = nc.tensor.transpose(ps[:, c * SP_:(c + 1) * SP_], ctx_n[:, c, k * P:(k + 1) * P],
                                                       ident[0:SP_, 0:SP_])
                    last.then_inc(unit_ready, 1)

                def project_k(it, m):
                    ps = open_unit(it, "K%d" % m)
                    if m == 0:
                        wait_emptied(pe, it, "X1", "D", back=1)
                    w = slice(m * P, (m + 1) * P)
                    in_three(ps[:, 0:SKE], [(wkv_hi[:, k, w], wkv_lo[:, k, w], ctxT_hi[:, k, :], ctxT_lo[:, k, :])
                                            for k in range(KC)]).then_inc(unit_ready, 1)

                def project_v(it, unit):
                    half, c = int(unit[1]), int(unit[2])
                    w = slice(INNER + half * 512, INNER + (half + 1) * 512)
                    ps = open_unit(it, unit)
                    s = slice(c * SP_, (c + 1) * SP_)
                    in_three(ps[0:SP_, :], [(ctxT_hi[:, k, s], ctxT_lo[:, k, s], wkv_hi[:, k, w], wkv_lo[:, k, w])
                                            for k in range(KC)]).then_inc(unit_ready, 1)

                def project_q(it, u):
                    ps = open_unit(it, "Q%d" % u)
                    if u == 0:
                        wait_emptied(pe, it, "Xx", "A", back=1)
                    for n in range(4):
                        m = 4 * u + n
                        for k in range(KC):
                            last = nc.tensor.matmul(ps[:, n * NQ:(n + 1) * NQ], wq[:, k, m * P:(m + 1) * P], xT[:, k, :],
                                                    start=k == 0, stop=k == KC - 1)
                    last.then_inc(unit_ready, 1)

                def qk(it, j):
                    if j == 0:
                        pe.wait_ge(q_ready, along(it, lambda i: 2 * (i + 1)))
                    for c in range(SC):
                        if later(it) or j:
                            pe.wait_ge(exp_done, along(it, lambda i: 12 * i + 3 * j + c - 3 + 1))
                        s = slice(c * SP_, (c + 1) * SP_)
                        for n in range(2):
                            m = 2 * j + n
                            last = in_three(scores[0:SP_, c, n * 2 * NQ:(n + 1) * 2 * NQ],
                                            [(k_hi[:, m, s], k_lo[:, m, s], q_hi[:, m, :], q_lo[:, m, :])])
                        last.then_inc(scores_ready, 1)

                def pv(it, j):
                    if j == 0 or j == 2:
                        for u in ("V01", "V02") if j == 0 else ("V10", "V12"):
                            wait_emptied(pe, it, u, readers(u), back=1)
                    if j >= 2:
                        wait_emptied(pe, it, "O%d" % (j - 2), "D")
                    elif j == 1 and later(it):
                        wait_emptied(pe, it, "O3", "D", back=1)
                    elif j == 0 and later(it):
                        wait_emptied(pe, it, "W", "Y", back=1)
                    elif j == 0:
                        wait_emptied(pe, it, "Xx", "A", back=1)
                    pe.wait_ge(clipped, along(it, lambda i: 12 * i + 3 * j + SC))
                    for h in range(4):
                        for c in range(SC):
                            last = nc.tensor.matmul(mixed[0:NQ, j % 2, h * D1:(h + 1) * D1],
                                                    probs[:, j % 2, c, h * NQ:(h + 1) * NQ], v[:, c, 4 * j + h, :],
                                                    start=c == 0, stop=c == SC - 1)
                    last.then_inc(mixed_ready, 1)

                def transpose_o(it, j):
                    ps = open_unit(it, "O%d" % j)
                    pe.wait_ge(o_normed, along(it, lambda i: 4 * i + j + 1))
                    for n in range(2):
                        m = 2 * j + n
                        last = nc.tensor.transpose(ps[:, n * NQ:(n + 1) * NQ], o[:, m * P:(m + 1) * P],
                                                   ident[0:NQ, 0:NQ])
                    last.then_inc(unit_ready, 1)

                def project_o(it, split):
                    ps = open_unit(it, "W")
                    if "Xx" in (STEADY if not isinstance(it, int) or it < LOOPED else LATE):
                        wait_emptied(pe, it, "Xx", "A")
                    if not later(it):
                        pe.wait_ge(wo_cut, 1)

                    def part(pairs):
                        return in_three(ps[0:NQ, 0:DIM], [(oT_hi[:, m, :], oT_lo[:, m, :], wo_hi[:, m, :], wo_lo[:, m, :])
                                                          for m in pairs],
                                        start=0 in pairs, stop=PAIRS - 1 in pairs)

                    if split:
                        wait_emptied(pe, it, "O2", "D")
                        part(range(PAIRS - 2))
                        transpose_o(it, QUADS - 1)
                    wait_emptied(pe, it, "O3", "D")
                    part(range(PAIRS - 2 if split else 0, PAIRS)).then_inc(unit_ready, 1)

                def iteration(it, project=True, transpose=True):
                    if not project:
                        qk(it, 0)
                    for j in range(QUADS):
                        if project:
                            qk(it, j)
                        elif j < QUADS - 1:
                            qk(it, j + 1)
                        if project:
                            project_k(it, 2 * j)
                            project_k(it, 2 * j + 1)
                        if j:
                            transpose_o(it, j - 1)
                        pv(it, j)
                        if project and j == 1:
                            for u in V_LOW:
                                project_v(it, u)
                    for u in tail_units(project, transpose):
                        if u[0] == "Q":
                            project_q(it, int(u[1]))
                        elif u[0] == "V":
                            project_v(it, u)
                        elif u[0] == "O":
                            if project:
                                transpose_o(it, 3)
                        elif u[0] == "X":
                            transposes(it, u, it + 2)
                        else:
                            project_o(it, split=not project)

                pe.wait_ge(ident_set, 2)
                for u in ("X0", "X1"):
                    transposes(-2, u, 0)
                pe.wait_ge(zeros_set, 3)
                for m in range(PAIRS):
                    if m % 4 == 0:
                        pe.wait_ge(tails, m // 4 + 1)
                    project_k(-1, m)
                    if m == 1:
                        transposes(-2, "Xx", 0)
                pe.wait_ge(wq_in, 16)
                project_q(-1, 0)
                project_q(-1, 1)
                for half, units in enumerate((V_LOW, V_HIGH)):
                    pe.wait_ge(tails, 2 + half + 1)
                    for u in units:
                        project_v(-1, u)
                        if u == "V10":
                            transposes(-1, "Xx", 1)
                for u in ("X0", "X1"):
                    transposes(-1, u, 1)
                iteration(0)
                with pe.Fori(1, LOOPED) as it:
                    iteration(it)
                iteration(LOOPED, transpose=False)
                iteration(LOOPED + 1, project=False, transpose=False)

            @block.scalar
            def _(act):
                def empty_x(it, unit):
                    wait_unit(act, it, unit)
                    ps = bank(it, unit)
                    if unit == "Xx":
                        for k in range(KC):
                            last = nc.scalar.activation(xT[:, k, :], ps[:, k * NQ:(k + 1) * NQ], ACT.Identity,
                                                        scale=lnl_w[:, k:k + 1], bias=lnl_b[:, k:k + 1])
                    else:
                        k = int(unit[1])
                        last = nc.scalar.activation(ctx_f[:, k, :], ps[:, 0:SK], ACT.Identity,
                                                    scale=lnc_w[:, k:k + 1], bias=lnc_b[:, k:k + 1])
                    last.then_inc(act_emptied, 1)

                def empty_k(it, m):
                    wait_unit(act, it, "K%d" % m)
                    nc.scalar.copy(k_hi[:, m, :], bank(it, "K%d" % m)[:, 0:SK]).then_inc(act_emptied, 1)

                def empty_v(it, u):
                    half, c = int(u[1]), int(u[2])
                    if readers(u) == "A":
                        wait_unit(act, it, u)
                        nc.scalar.copy(v[:, c, 8 * half:8 * half + 8, 0:D],
                                       bank(it, u)[0:SP_, :].rearrange("p (h d) -> p h d", d=D)
                                       ).then_inc(act_emptied, 1)

                def empty_q(it, u):
                    wait_unit(act, it, "Q%d" % u)
                    if u or not isinstance(it, int) or it >= 0:
                        act.wait_ge(q_ready, along(it, lambda i: 2 * (i + 1) + u))
                    nc.scalar.copy(q_full[:], bank(it, "Q%d" % u)[:, 0:4 * NQ]).then_inc(act_emptied, 1)

                def empty_o(it, j):
                    wait_unit(act, it, "O%d" % j)
                    nc.scalar.copy(oT_hi[:, 2 * j:2 * j + 2, :],
                                   bank(it, "O%d" % j)[:, 0:2 * NQ].rearrange("p (m n) -> p m n", n=NQ)
                                   ).then_inc(act_emptied, 1)

                def exps(it, j):
                    for c in range(SC):
                        act.wait_ge(scores_ready, along(it, lambda i: 12 * i + 3 * j + c + 1))
                        nc.scalar.activation(probs[:, j % 2, c, :], scores[0:SP_, c, 0:4 * NQ], ACT.Exp
                                             ).then_inc(exp_done, 1)

                def load_residual(it):
                    if later(it):
                        act.wait_ge(y_ready, along(it, lambda i: i))
                    act.dma_start(x_res[:], io["x"][it]).then_inc(res_loaded, 16)

                def store(it):
                    act.wait_ge(y_ready, along(it, lambda i: i + 1))
                    act.dma_start(x1[it], y).then_inc(stored, 16)

                def iteration(it, project=True, transpose=True):
                    for j in range(QUADS):
                        exps(it, j)
                        if j == 0:
                            load_residual(it)
                        if j == 1 and later(it):
                            store(it - 1)
                        if project:
                            empty_k(it, 2 * j)
                            empty_k(it, 2 * j + 1)
                        if j:
                            empty_o(it, j - 1)
                        if project and j == 1:
                            for u in V_LOW:
                                empty_v(it, u)
                    for u in tail_units(project, transpose):
                        if u[0] == "Q":
                            empty_q(it, int(u[1]))
                        elif u[0] == "V":
                            empty_v(it, u)
                        elif u[0] == "O":
                            empty_o(it, 3)
                        elif u[0] == "X":
                            empty_x(it, u)

                def head(n):
                    act.wait_ge((kv_in + [wo_in])[n], 16)
                    w = slice(n * KV_COLS, (n + 1) * KV_COLS)
                    if n < KV_PARTS:
                        nc.scalar.copy(wkv_hi[:, :, w], raw_kv[:, :, w]).then_inc(heads, 1)
                    else:
                        nc.scalar.copy(wo_hi[:], raw_o[:]).then_inc(heads, 1)

                for t, name in ((lnl_w, "lnl_w"), (lnl_b, "lnl_b"), (lnc_w, "lnc_w"), (lnc_b, "lnc_b")):
                    act.dma_start(t[:], io[name]).then_inc(small_in, 16)
                head(0)
                act.wait_ge(small_in, 64)
                nc.scalar.mul(lnl_w[:], lnl_w[:], float(D) ** -0.5).then_inc(scaled, 1)
                nc.scalar.mul(lnl_b[:], lnl_b[:], float(D) ** -0.5).then_inc(scaled, 1)
                act.wait_ge(scaled, 2)
                for u in ("X0", "X1"):
                    empty_x(-2, u)
                for m in range(PAIRS):
                    if m >= PAIRS - 2:
                        head(m - (PAIRS - 2) + 2)
                    empty_k(-1, m)
                    if m == 0:
                        head(1)
                    if m == 1:
                        empty_x(-2, "Xx")
                empty_q(-1, 0)
                empty_q(-1, 1)
                for u in V_LOW + V_HIGH:
                    empty_v(-1, u)
                    if u == "V02":
                        head(KV_PARTS)
                    if u == "V10":
                        empty_x(-1, "Xx")
                for u in ("X0", "X1"):
                    empty_x(-1, u)
                iteration(0)
                with act.Fori(1, LOOPED) as it:
                    iteration(it)
                iteration(LOOPED, transpose=False)
                iteration(LOOPED + 1, project=False, transpose=False)
                store(LOOPED + 1)
                act.wait_ge(rows_normed, RS)

            @block.vector
            def _(dve):
                def take_stats(b):
                    n = lambda k: along(b, lambda i: (SC + 1) * i + k, B - 1)
                    dve.wait_ge(ctx_loaded, along(b, lambda i: 16 * (i + 1), B - 1))
                    dve.wait_ge(x_loaded, along(b, lambda i: 16 * (i + 1), B - 1))
                    for c in range(SC):
                        nc.vector.bn_stats(stats[0:SP_, c, :], ctx_in[:, c, :]).then_inc(stats_done, 1)
                    nc.vector.bn_stats(stats[0:NQ, SC, :], x_in[:]).then_inc(stats_done, 1)
                    dve.wait_ge(stats_done, n(SC + 1))
                    nc.vector.memset(idle[:], 0.0)
                    for c in range(SC + 1):
                        r = SP_ if c < SC else NQ
                        nc.vector.bn_aggr(mv[0:r, c, :], stats[0:r, c, :]).then_inc(mv_ready, 1)

                def normalise_ctx():
                    for c in range(SC):
                        nc.vector.tensor_scalar(ctx_n[:, c, :], ctx_in[:, c, :], mv[0:SP_, c, 0:1], rstd[0:SP_, c, :],
                                                ALU.subtract, ALU.mult).then_inc(ctx_normed, 1)

                def normalise(b, it):
                    one = along(b, lambda i: i + 1, B - 1)
                    dve.wait_ge(rstd_ready, one)
                    if isinstance(it, int) and it == -2:
                        normalise_ctx()
                    nc.vector.tensor_scalar(x_n1[:], x_in[:], mv[0:NQ, SC, 0:1], rstd[0:NQ, SC, :], ALU.subtract,
                                            ALU.mult).then_inc(x_normed1, 1)
                    dve.wait_ge(x_normed1, one)
                    nc.vector.bn_stats(x_stats[0:NQ, :], x_n1[:]).then_inc(x_stats_done, 1)
                    dve.wait_ge(x_stats_done, one)
                    nc.vector.memset(idle[:], 0.0)
                    nc.vector.bn_aggr(x_mv[0:NQ, 0, :], x_stats[0:NQ, :]).then_inc(x_mv_ready, 1)
                    if not isinstance(it, int) or it > -2:
                        wait_unit(dve, it, "X1", back=1)
                        normalise_ctx()

                def normalise_x_again(b):
                    dve.wait_ge(x_rstd_ready, along(b, lambda i: i + 1, B - 1))
                    nc.vector.tensor_scalar(x_n2[:], x_n1[:], x_mv[0:NQ, 0, 0:1], x_rstd[0:NQ, 0, :], ALU.subtract,
                                            ALU.mult).then_inc(x_normed2, 1)

                def split_x(it, u):
                    k = int(u[1])
                    wait_emptied(dve, it, u, "A")
                    nc.vector.tensor_copy(ctxT_hi[:, k, 0:SK], ctx_f[:, k, :]).then_inc(head_done, 1)
                    dve.wait_ge(head_done, along(it, lambda i: KC * (i + 2) + k + 1))
                    nc.vector.tensor_tensor(ctxT_lo[:, k, 0:SK], ctx_f[:, k, :], ctxT_hi[:, k, 0:SK],
                                            ALU.subtract).then_inc(dve_emptied, 1)

                def tail_k(it, m):
                    u = "K%d" % m
                    wait_emptied(dve, it, u, "A")
                    nc.vector.tensor_tensor(k_lo[:, m, :], bank(it, u)[:, 0:SK], k_hi[:, m, :],
                                            ALU.subtract).then_inc(dve_emptied, 1)

                def empty_v(it, u):
                    half, c = int(u[1]), int(u[2])
                    if readers(u) == "D":
                        wait_unit(dve, it, u)
                        nc.vector.tensor_copy(v[:, c, 8 * half:8 * half + 8, 0:D],
                                              bank(it, u)[0:SP_, :].rearrange("p (h d) -> p h d", d=D)
                                              ).then_inc(dve_emptied, 1)

                def q_parts(n):
                    return [(slice(e * D, (e + 1) * D), slice(4 * n, 4 * n + 4), slice(e * NQ, (e + 1) * NQ))
                            for e in range(2)]

                full = q_full[:].rearrange("p (m n) -> p m n", n=NQ)

                def head_q(it, n):
                    wait_emptied(dve, it, "Q%d" % n, "A")
                    for s in q_parts(n):
                        nc.vector.tensor_copy(q_hi[s], full[s[0]]).then_inc(q_heads, 1)

                def tail_q(it, n):
                    dve.wait_ge(q_heads, along(it, lambda i: 4 * (i + 1) + 2 * n + 2))
                    for s in q_parts(n):
                        last = nc.vector.tensor_tensor(q_lo[s], full[s[0]], q_hi[s], ALU.subtract)
                    last.then_inc(q_ready, 1)

                def tail_o(it, j):
                    u = "O%d" % j
                    wait_emptied(dve, it, u, "A")
                    ps = bank(it, u)[:, 0:2 * NQ].rearrange("p (m n) -> p m n", n=NQ)
                    nc.vector.tensor_tensor(oT_lo[:, 2 * j:2 * j + 2, :], ps, oT_hi[:, 2 * j:2 * j + 2, :],
                                            ALU.subtract).then_inc(dve_emptied, 1)

                def clip(it, j):
                    for c in range(SC):
                        dve.wait_ge(exp_done, along(it, lambda i: 12 * i + 3 * j + c + 1))
                        nc.vector.tensor_scalar(probs[:, j % 2, c, :], probs[:, j % 2, c, :], float(np.exp(-CLIP)),
                                                float(np.exp(CLIP)), ALU.max, ALU.min).then_inc(clipped, 1)

                def norm_o(it, j):
                    q = along(it, lambda i: 4 * i + j + 1)
                    dve.wait_ge(mixed_ready, q)
                    ps = mixed[0:NQ, j % 2, 0:4 * D1].rearrange("p (h d) -> p h d", d=D1)
                    nc.vector.reciprocal(rden[:], ps[:, :, D:D1]).then_inc(rden_ready, 1)
                    dve.wait_ge(rden_ready, q)
                    nc.vector.tensor_tensor(o[:, 4 * j * D:4 * (j + 1) * D].rearrange("p (h d) -> p h d", d=D),
                                            ps[:, :, 0:D], rden[:].to_broadcast([NQ, 4, D]), ALU.mult
                                            ).then_inc(o_normed, 1)

                def finish(it):
                    wait_unit(dve, it, "W")
                    dve.wait_ge(residual_ready, along(it, lambda i: i + 1))
                    if later(it):
                        dve.wait_ge(stored, along(it, lambda i: 16 * i))
                    nc.vector.tensor_tensor(y, bank(it, "W")[0:NQ, 0:DIM], x_res[:], ALU.add).then_inc(y_ready, 1)

                def look_at_piece(n):
                    one = along(n, lambda i: i + 1)
                    dve.wait_ge(piece_in, along(n, lambda i: 16 * (i + 1)))
                    nc.vector.tensor_scalar(low_bits[:], piece[:], LOW_BITS, None, ALU.bitwise_and
                                            ).then_inc(piece_masked, 1)
                    dve.wait_ge(piece_masked, one)
                    nc.vector.tensor_reduce(piece_low[:], low_bits[:], mybir.AxisListType.X, ALU.max
                                            ).then_inc(piece_reduced, 1)
                    dve.wait_ge(piece_reduced, one)
                    nc.vector.tensor_tensor(low_seen[:], low_seen[:], piece_low[:], ALU.max).then_inc(piece_seen, 1)

                def stats_of_first_rows():
                    dve.wait_ge(rows_in, 16)
                    for r in range(RS):
                        nc.vector.bn_stats(stats[:, r, :], first_rows[:, r, :]).then_inc(stats_done, 1)
                    dve.wait_ge(stats_done, (SC + 1) * B + RS)
                    for r in range(RS):
                        nc.vector.bn_aggr(mv[:, r, :], stats[:, r, :]).then_inc(mv_ready, 1)

                def normalise_first_rows():
                    dve.wait_ge(rstd_ready, B + 1)
                    for r in range(RS):
                        nc.vector.tensor_scalar(first_rows[:, r, :], first_rows[:, r, :], mv[:, r, 0:1],
                                                rstd[:, r, :], ALU.subtract, ALU.mult).then_inc(rows_normed, 1)

                def iteration(it, project=True, transpose=True):
                    for j in range(QUADS):
                        clip(it, j)
                        if project and not transpose and j == 3:
                            stats_of_first_rows()
                        if not project and j == 0:
                            normalise_first_rows()
                        if j == 3 and transpose:
                            look_at_piece(it)
                        if project:
                            tail_k(it, 2 * j)
                            tail_k(it, 2 * j + 1)
                        if j:
                            tail_o(it, j - 1)
                        if transpose:
                            if j == 0:
                                take_stats(it + 2)
                            if j == 1:
                                normalise(it + 2, it)
                            if j == 2:
                                normalise_x_again(it + 2)
                        norm_o(it, j)
                        if project and j == 1:
                            for u in V_LOW:
                                empty_v(it, u)
                    for u in tail_units(project, transpose):
                        if u[0] == "Q":
                            head_q(it, int(u[1]))
                        if u == "Q0":
                            tail_q(it, 0)
                        elif u[0] == "V":
                            empty_v(it, u)
                        elif u[0] == "O":
                            tail_o(it, 3)
                            if project:
                                tail_q(it, 1)
                        elif u in ("X0", "X1"):
                            split_x(it, u)
                        elif u == "W":
                            finish(it)

                def tail(n):
                    dve.wait_ge(heads, n + 1)
                    w = slice(n * KV_COLS, (n + 1) * KV_COLS)
                    nc.vector.tensor_tensor(wkv_lo[:, :, w], raw_kv[:, :, w], wkv_hi[:, :, w], ALU.subtract
                                            ).then_inc(tails, 1)

                nc.vector.memset(mv[:], 1.0).then_inc(ones_set, 1)
                nc.vector.memset(x_mv[:], 1.0).then_inc(ones_set, 1)
                nc.vector.memset(low_seen[:], 0.0).then_inc(ones_set, 1)
                for k, c in enumerate((EPS, -0.5, 1.5)):
                    nc.vector.memset(const[:, :, k:k + 1], c).then_inc(ones_set, 1)
                dve.wait_ge(ones_set, 6)
                take_stats(0)
                normalise(0, -2)
                tail(0)
                split_x(-2, "X0")
                split_x(-2, "X1")
                normalise_x_again(0)
                for m in range(PAIRS):
                    if m == PAIRS - 1:
                        tail(2)
                    tail_k(-1, m)
                    if m == 1:
                        tail(1)
                    if m == 0:
                        take_stats(1)
                    if m == 4:
                        normalise(1, -1)
                normalise_x_again(1)
                dve.wait_ge(zeros_set, 5)
                for n in range(2):
                    head_q(-1, n)
                    tail_q(-1, n)
                    if n == 0:
                        tail(3)
                for u in V_LOW + V_HIGH:
                    empty_v(-1, u)
                split_x(-1, "X0")
                split_x(-1, "X1")
                iteration(0)
                with dve.Fori(1, LOOPED) as it:
                    iteration(it)
                iteration(LOOPED, transpose=False)
                iteration(LOOPED + 1, project=False, transpose=False)

        return stored, early, low_seen, ones, ident, first_rows, ff_scales


T_UNITS = ["T%d" % r for r in range(RS)]
F_TILE = ([g + str(m) for m in range(HC) for g in "GH"] + ["M%d" % m for m in range(HC)]
          + ["N%d" % m for m in range(HC)] + T_UNITS + ["F%d" % r for r in range(RS)])
F_LAST = [u for u in F_TILE if u not in T_UNITS]
F_ORDER = T_UNITS + F_TILE * (TILES - 1) + F_LAST


def f_readers(unit):
    return {"T": "AD", "G": "A", "H": "D", "M": "A", "N": "A", "F": "D"}[unit[0]]


F_BEFORE = {e: prefix(F_ORDER, e, f_readers) for e in "AD"}
GATED, MIDDLE, LAST = 0, HC, 2 * HC
HIDDEN = 3 * HC


def f_place(t, unit):
    if t == -1:
        return T_UNITS.index(unit)
    return len(T_UNITS) + len(F_TILE) * t + (F_TILE if t < TILES - 1 else F_LAST).index(unit)


def feed_forward(nc, io, x1, ff_copy, x1_stored, early, low_seen, ones, ident, first_rows, ff_scales, out):
    with ExitStack() as ctx:
        def sb(name, shape, dt=F32):
            return ctx.enter_context(nc.sbuf_tensor(name, shape, dt))

        def sem(name):
            return ctx.enter_context(nc.semaphore(name))

        late = sb("ff_late", [P, (PIECES - EARLY_PIECES) * PIECE])
        s1, s2, t1, t2 = ff_scales
        s3_rows = sb("s3_rows", [P, DIM])
        inexact = sb("inexact", [1, 1], I32)
        x_in = sb("f_x_in", [P, RS, DIM])
        x_res = sb("f_x_res", [P, RS, DIM])
        x_n = sb("f_x_n", [P, RS, DIM])
        stats = sb("f_stats", [P, RS, 6])
        mv = sb("f_mv", [P, RS, 2])
        rstd = sb("f_rstd", [P, RS, 1])
        const = sb("f_const", [P, RS, 3])
        work = sb("f_work", [P, RS, 3])
        idle = sb("f_idle", [P, 1])
        xT = [sb("f_xT_hi", [P, KC, TR], F32R), sb("f_xT_lo", [P, KC, TR], F32R)]
        act_a = [sb("act_a_hi", [P, HC, TR], F32R), sb("act_a_lo", [P, HC, TR], F32R)]
        act_b = [sb("act_b_hi", [P, HC, TR], F32R), sb("act_b_lo", [P, HC, TR], F32R)]
        gate = sb("gate", [P, 2, TR])
        full = sb("full", [P, 2, TR])
        y = sb("f_y", [P, RS, DIM])
        banks = ctx.enter_context(nc.psum_tensor("banks", [P, 8, 512], F32))

        def weights(tile, first, name, chunks):
            return tile[:, first:first + W_COLS[name]].rearrange("p (k n) -> p k n", k=chunks)

        w1 = weights(early, 0, "w1", KC)
        w2 = weights(early, W_COLS["w1"], "w2", KC)
        h1 = weights(early, W_COLS["w1"] + W_COLS["w2"], "h1", HC)
        h2 = weights(late, 0, "h2", HC)
        w3 = weights(late, W_COLS["h2"], "w3", HC)

        late_in, s3_in = sem("late_in"), sem("s3_in")
        f_const_set = sem("f_const_set")
        low_sum, inexact_set = sem("low_sum"), sem("inexact_set")
        x_loaded, res_loaded = sem("f_x_loaded"), sem("f_res_loaded")
        stats_done, mv_ready, rstd_ready = sem("f_stats_done"), sem("f_mv_ready"), sem("f_rstd_ready")
        x_normed, newton = sem("f_x_normed"), sem("f_newton")
        unit_ready, act_emptied, dve_emptied = sem("f_unit_ready"), sem("f_act_emptied"), sem("f_dve_emptied")
        gated_heads, hidden_heads = sem("gated_heads"), sem("hidden_heads")
        hidden_ready = sem("hidden_ready")
        summed, stored = sem("f_summed"), sem("f_stored")
        emptied = {"A": act_emptied, "D": dve_emptied}
        x_tiles, out_tiles = row_tiles(x1), row_tiles(out)

        def over(t, f):
            return along(t, f, TILES - 2)

        def bank(t, unit):
            return banks[:, f_place(t if isinstance(t, int) else 1, unit) % 8, :]

        def wait_unit(eng, t, unit):
            eng.wait_ge(unit_ready, over(t, lambda i: f_place(i, unit) + 1))

        def wait_emptied(eng, t, unit, engine, back=0):
            eng.wait_ge(emptied[engine], over(t, lambda i: F_BEFORE[engine][f_place(i - back, unit) + 1]))

        def wait_hidden(eng, t, n):
            eng.wait_ge(hidden_ready, over(t, lambda i: HIDDEN * i + n + 1))

        with nc.Block() as block:
            @block.sync
            def _(sp):
                sp.dma_start(in_pieces(late[:]), ff_copy[EARLY_PIECES:PIECES].rearrange("n p c -> p n c")).then_inc(late_in, 16)
                sp.dma_start(x_res[:], x_tiles[0]).then_inc(res_loaded, 16)
                sp.wait_ge(x1_stored, 16 * B)
                sp.dma_start(x_in[:], x_tiles[1]).then_inc(x_loaded, 16)
                with sp.Fori(1, TILES - 1) as t:
                    sp.wait_ge(x_normed, over(t, lambda i: RS * i))
                    sp.dma_start(x_in[:], x_tiles[t + 1]).then_inc(x_loaded, 16)
                    sp.wait_ge(summed, over(t, lambda i: RS * i))
                    sp.dma_start(x_res[:], x_tiles[t]).then_inc(res_loaded, 16)
                sp.wait_ge(summed, RS * (TILES - 1))
                sp.dma_start(x_res[:], x_tiles[TILES - 1]).then_inc(res_loaded, 16)

            @block.gpsimd
            def _(pool):
                def roots(t):
                    pool.wait_ge(mv_ready, along(t, lambda i: RS * i, TILES - 1))
                    inverse_root(nc, pool, rstd[:], mv[:, :, 1:2], [const[:, :, k:k + 1] for k in range(3)],
                                 [work[:, :, k:k + 1] for k in range(3)], newton,
                                 along(t, lambda i: NEWTON_OPS * (i - 1), TILES - 1), rstd_ready)

                for k, c in enumerate((EPS, -0.5, 1.5)):
                    nc.gpsimd.memset(const[:, :, k:k + 1], c).then_inc(f_const_set, 1)
                pool.wait_ge(f_const_set, 3)
                with pool.Fori(1, TILES) as t:
                    roots(t)

            @block.tensor
            def _(pe):
                def open_unit(t, unit):
                    g = f_place(t if isinstance(t, int) else 1, unit)
                    if g >= 8:
                        e = f_readers(F_ORDER[g - 8])[-1]
                        pe.wait_ge(emptied[e], over(t, lambda i: F_BEFORE[e][f_place(i, unit) - 7]))
                    return bank(t, unit)

                def transposes(t, r):
                    ps = open_unit(t, "T%d" % r)
                    if isinstance(t, int) and t == -1:
                        rows = first_rows
                    else:
                        rows = x_n
                        pe.wait_ge(x_normed, over(t, lambda i: RS * i + r + 1))
                    for k in range(KC):
                        last = nc.tensor.transpose(ps[:, k * P:(k + 1) * P], rows[:, r, k * P:(k + 1) * P], ident[:])
                    last.then_inc(unit_ready, 1)

                def tiles(exact):
                    def w_of(ap):
                        return ap.bitcast(F32R) if exact else ap

                    def x_of(ap):
                        return ap if exact else ap.bitcast(F32)

                    def hidden(t, name, m, w, source, chunks, ready):
                        ps = open_unit(t, name + str(m))
                        for k in range(chunks):
                            if ready is not None:
                                wait_hidden(pe, t, ready + k)
                            for part in range(2):
                                last = nc.tensor.matmul(ps, w_of(w[:, k, m * P:(m + 1) * P]), x_of(source[part][:, k, :]),
                                                        start=k + part == 0, stop=k == chunks - 1 and part == 1)
                        last.then_inc(unit_ready, 1)

                    def down(t, r):
                        ps = open_unit(t, "F%d" % r)
                        for k in range(HC):
                            if r == 0:
                                wait_hidden(pe, t, LAST + k)
                            for part in range(2):
                                last = nc.tensor.matmul(ps[:, 0:DIM], x_of(act_a[part][:, k, r * P:(r + 1) * P]),
                                                        w_of(w3[:, k, :]), start=k + part == 0,
                                                        stop=k == HC - 1 and part == 1)
                        last.then_inc(unit_ready, 1)

                    def tile(t, more=True):
                        first = isinstance(t, int) and t == 0
                        wait_emptied(pe, t, "T%d" % (RS - 1), "D", back=1)
                        for m in range(HC):
                            hidden(t, "G", m, w1, xT, KC, None)
                            hidden(t, "H", m, w2, xT, KC, None)
                        for m in range(HC):
                            hidden(t, "M", m, h1, act_a, HC, GATED if m == 0 else None)
                        if first:
                            pe.wait_ge(late_in, 16)
                        for m in range(HC):
                            hidden(t, "N", m, h2, act_b, HC, MIDDLE if m == 0 else None)
                        if more:
                            for r in range(RS):
                                transposes(t, r)
                        for r in range(RS):
                            down(t, r)

                    tile(0)
                    with pe.Fori(1, TILES - 1) as t:
                        tile(t)
                    tile(TILES - 1, more=False)

                nc.tensor.matmul(banks[0:1, 7, 0:1], low_seen[:], ones[:], start=True, stop=True).then_inc(low_sum, 1)
                for r in range(RS):
                    transposes(-1, r)
                pe.wait_ge(inexact_set, 1)
                low = pe.value_load(inexact[0:1, 0:1])
                with pe.If(low > 0):
                    tiles(exact=False)
                with pe.Else():
                    tiles(exact=True)

            @block.scalar
            def _(act):
                act.dma_start(s3_rows[:], io["s3"].partition_broadcast(P)).then_inc(s3_in, 16)

                def empty_t(t, r):
                    wait_unit(act, t, "T%d" % r)
                    nc.scalar.copy(xT[0][:, :, r * P:(r + 1) * P],
                                   bank(t, "T%d" % r)[:, 0:KC * P].rearrange("p (k n) -> p k n", n=P)
                                   ).then_inc(act_emptied, 1)

                def silu(t, m):
                    wait_unit(act, t, "G%d" % m)
                    if later(t) or m >= 2:
                        act.wait_ge(dve_emptied, over(t, lambda i: F_BEFORE["D"][f_place(
                            i if m >= 2 else i - 1, "H%d" % ((m - 2) % HC)) + 1]))
                    nc.scalar.activation(gate[:, m % 2, :], bank(t, "G%d" % m), ACT.Silu,
                                         scale=s1[:, m:m + 1]).then_inc(act_emptied, 1)

                def gated_head(t, m):
                    wait_emptied(act, t, "H%d" % m, "D")
                    nc.scalar.copy(act_a[0][:, m, :], full[:, m % 2, :]).then_inc(gated_heads, 1)

                def tile(t, more=True):
                    silu(t, 0)
                    for m in range(1, HC):
                        silu(t, m)
                        gated_head(t, m - 1)
                    gated_head(t, HC - 1)
                    for name, s, stage in (("M", t1, MIDDLE), ("N", t2, LAST)):
                        for m in range(HC):
                            wait_unit(act, t, name + str(m))
                            wait_hidden(act, t, stage + m - 2)
                            nc.scalar.activation(full[:, m % 2, :], bank(t, name + str(m)), ACT.Gelu,
                                                 scale=s[:, m:m + 1]).then_inc(act_emptied, 1)
                    if more:
                        for r in range(RS):
                            empty_t(t, r)
                    for part in [slice(0, RS)] if more else [slice(r, r + 1) for r in range(RS)]:
                        act.wait_ge(summed, over(t, lambda i: RS * i + part.stop))
                        act.dma_start(out_tiles[t][:, part, :], y[:, part, :]).then_inc(stored, 16)

                for r in range(RS):
                    empty_t(-1, r)
                tile(0)
                with act.Fori(1, TILES - 1) as t:
                    tile(t)
                tile(TILES - 1, more=False)
                act.wait_ge(stored, 16 * (TILES - 1 + RS))

            @block.vector
            def _(dve):
                def normalise(t, turn):
                    n = lambda k: along(t, lambda i: RS * (i - 1) + k, TILES - 1)
                    dve.wait_ge(x_loaded, along(t, lambda i: 16 * i, TILES - 1))
                    for r in range(RS):
                        nc.vector.bn_stats(stats[:, r, :], x_in[:, r, :]).then_inc(stats_done, 1)
                    dve.wait_ge(stats_done, n(RS))
                    nc.vector.memset(idle[:], 0.0)
                    for r in range(RS):
                        nc.vector.bn_aggr(mv[:, r, :], stats[:, r, :]).then_inc(mv_ready, 1)
                    dve.wait_ge(rstd_ready, along(t, lambda i: i, TILES - 1))
                    dve.wait_ge(unit_ready, over(turn, lambda i: f_place(i - 1, "T%d" % (RS - 1)) + 1))
                    for r in range(RS):
                        nc.vector.tensor_scalar(x_n[:, r, :], x_in[:, r, :], mv[:, r, 0:1], rstd[:, r, :],
                                                ALU.subtract, ALU.mult).then_inc(x_normed, 1)

                def tail_t(t, r):
                    wait_emptied(dve, t, "T%d" % r, "A")
                    s = slice(r * P, (r + 1) * P)
                    nc.vector.tensor_tensor(xT[1][:, :, s], bank(t, "T%d" % r)[:, 0:KC * P].rearrange(
                        "p (k n) -> p k n", n=P), xT[0][:, :, s], ALU.subtract).then_inc(dve_emptied, 1)

                def gated(t, m):
                    wait_unit(dve, t, "H%d" % m)
                    wait_emptied(dve, t, "G%d" % m, "A")
                    if later(t) or m >= 2:
                        wait_hidden(dve, t, m - 2)
                    nc.vector.scalar_tensor_tensor(out=full[:, m % 2, :], in0=bank(t, "H%d" % m), scalar=s2[:, m:m + 1],
                                                   in1=gate[:, m % 2, :], op0=ALU.mult, op1=ALU.mult
                                                   ).then_inc(dve_emptied, 1)

                def gated_tail(t, m):
                    dve.wait_ge(gated_heads, over(t, lambda i: HC * i + m + 1))
                    nc.vector.tensor_tensor(act_a[1][:, m, :], full[:, m % 2, :], act_a[0][:, m, :], ALU.subtract
                                            ).then_inc(hidden_ready, 1)

                def tile(t, more=True):
                    gated(t, 0)
                    for m in range(1, HC):
                        gated(t, m)
                        gated_tail(t, m - 1)
                    gated_tail(t, HC - 1)
                    for name, dst, stage in (("M", act_b, 0), ("N", act_a, 1)):
                        for m in range(HC):
                            wait_emptied(dve, t, name + str(m), "A")
                            nc.vector.tensor_copy(dst[0][:, m, :], full[:, m % 2, :]).then_inc(hidden_heads, 1)
                            dve.wait_ge(hidden_heads, over(t, lambda i: 2 * HC * i + HC * stage + m + 1))
                            nc.vector.tensor_tensor(dst[1][:, m, :], full[:, m % 2, :], dst[0][:, m, :], ALU.subtract
                                                    ).then_inc(hidden_ready, 1)
                        if more and stage == 0:
                            normalise(t + 1, t)
                    if more:
                        for r in range(RS):
                            tail_t(t, r)
                    if later(t):
                        dve.wait_ge(stored, over(t, lambda i: 16 * i))
                    else:
                        dve.wait_ge(s3_in, 16)
                    dve.wait_ge(res_loaded, over(t, lambda i: 16 * (i + 1)))
                    for r in range(RS):
                        wait_unit(dve, t, "F%d" % r)
                        nc.vector.tensor_tensor(y[:, r, :], bank(t, "F%d" % r)[:, 0:DIM], s3_rows[:], ALU.mult
                                                ).then_inc(dve_emptied, 1)
                        wait_emptied(dve, t, "F%d" % r, "D")
                        nc.vector.tensor_tensor(y[:, r, :], y[:, r, :], x_res[:, r, :], ALU.add).then_inc(summed, 1)

                dve.wait_ge(low_sum, 1)
                nc.vector.tensor_copy(inexact[:], banks[0:1, 7, 0:1]).then_inc(inexact_set, 1)
                for r in range(RS):
                    tail_t(-1, r)
                tile(0)
                with dve.Fori(1, TILES - 1) as t:
                    tile(t)
                tile(TILES - 1, more=False)


def program(nc, io, out):
    x1 = nc.dram_tensor("x1", [B, NQ, DIM], F32, kind="Internal").ap()
    ff_copy = nc.dram_tensor("ff_copy", [PIECES, P, PIECE], F32, kind="Internal").ap()
    with ExitStack() as outlast:
        kept = attention(nc, io, x1, ff_copy, outlast)
        feed_forward(nc, io, x1, ff_copy, *kept, out)


def kernel(**inputs):
    import concourse.bacc as bacc
    from concourse.bass_utils import run_bass_kernel_spmd

    a = {k: np.asarray(w) for k, w in inputs.items()}

    def chunked(w):
        return w.reshape(-1, P, w.shape[-1]).transpose(1, 0, 2)

    xa, ff = "L0_xattn_", "L0_ffn_"
    side_by_side = np.concatenate([chunked(a[ff + n + "_w"].T).reshape(P, -1) for n in W_COLS], 1)
    side_by_side = np.pad(side_by_side, ((0, 0), (0, PIECES * PIECE - side_by_side.shape[1])))
    arrays = {
        "x": a["x"],
        "ctx": a["ctx_1024"].reshape(B, SC, SP_, DIM).transpose(0, 2, 1, 3),
        "lnl_w": a[xa + "ln_l_w"].reshape(KC, P).T, "lnl_b": a[xa + "ln_l_b"].reshape(KC, P).T,
        "lnc_w": a[xa + "ln_c_w"].reshape(KC, P).T, "lnc_b": a[xa + "ln_c_b"].reshape(KC, P).T,
        "wq": chunked(a[xa + "Wq"]), "wkv": a[xa + "Wkv"].reshape(KC, P, 2 * INNER), "wo": chunked(a[xa + "Wo"]),
        "bo": a[xa + "bo"],
        "ff": side_by_side.reshape(P, PIECES, PIECE).transpose(1, 0, 2),
        "s1": a[ff + "w1_s"].reshape(HC, P).T, "s2": a[ff + "w2_s"].reshape(HC, P).T,
        "t1": a[ff + "h1_s"].reshape(HC, P).T, "t2": a[ff + "h2_s"].reshape(HC, P).T,
        "s3": a[ff + "w3_s"],
    }
    nc = bacc.Bacc("TRN2", target_bir_lowering=False, num_devices=1)
    io, feeds = {}, {}
    for name, w in arrays.items():
        w = np.ascontiguousarray(w)
        feeds["in_" + name + "_dram"] = w
        io[name] = nc.dram_tensor("in_" + name + "_dram", w.shape, mybir.dt.from_np(w.dtype), kind="ExternalInput").ap()
    out = nc.dram_tensor("out_dram", [B, NQ, DIM], F32, kind="ExternalOutput").ap()
    program(nc, io, out)
    result = run_bass_kernel_spmd(nc, [feeds], core_ids=[0])
    return result.results[0]["out_dram"]
```
